# Optimizing a Trainium2 kernel written in Bass

```python
import numpy as np
import jax
import jax.numpy as jnp

def _softmax(x, axis=-1):
    return jax.nn.softmax(x, axis=axis)

def _gelu(x):
    return jax.nn.gelu(x, approximate=True)

def _silu(x):
    return jax.nn.silu(x)

def _sigmoid(x):
    return jax.nn.sigmoid(x)

def _layernorm(x, axis=-1, eps=1e-05):
    m = jnp.mean(x, axis=axis, keepdims=True)
    v = jnp.var(x, axis=axis, keepdims=True)
    return (x - m) / jnp.sqrt(v + eps)

def _scatter_add(tgt, idx, src, axis=0):
    return tgt.at[idx].add(src)

def _segment_sum(src, seg, n):
    return jax.ops.segment_sum(src, seg, n)
kernel_name = 'mk_decoder_preln_d2_seqx_r4_0ae1ba'

def setup_inputs(seed: int=0):
    np.random.seed(seed)
    _w = jnp.asarray

    def _rec_inputs():
        import jax
        import jax.numpy as jnp
        _rk = jax.random.key(seed)
        x = 7.22e-05 + 1 * jax.random.normal(jax.random.fold_in(_rk, 1), (2, 1024, 256), jnp.float32)
        _lenS = 1024 - jax.random.randint(jax.random.fold_in(_rk, 7), (2,), 0, max(1, 1024 // 4) + 1, jnp.int32)
        _lenS2 = 77 - jax.random.randint(jax.random.fold_in(_rk, 8), (2,), 0, max(1, 77 // 4) + 1, jnp.int32)
        _ctx_1024P = jax.random.normal(jax.random.fold_in(_rk, 11), (2, 16, 256), jnp.float32)
        _ctx_1024c = jax.random.dirichlet(jax.random.fold_in(_rk, 511), 0.3 * jnp.ones((16,), jnp.float32), (2, 77))
        _ctx_1024t = jnp.einsum('bsk,bkd->bsd', _ctx_1024c, _ctx_1024P)
        _ctx_1024t = _ctx_1024t * jax.lax.rsqrt(jnp.mean(jnp.square(_ctx_1024t)) + 1e-12) * 0.953939
        ctx_1024 = 4.13588e-05 + 0.999923 * (_ctx_1024t + 0.3 * jax.random.normal(jax.random.fold_in(_rk, 611), (2, 77, 256), jnp.float32))
        _validS = jnp.arange(1024)[None, :] < _lenS[:, None]
        _validS2 = jnp.arange(77)[None, :] < _lenS2[:, None]
        _causal = jnp.tril(jnp.ones((1024, 1024), dtype=bool))
        mask_BxS2_bf0 = jnp.logical_not(jnp.ones((2, 77), dtype=bool))
        return (x, ctx_1024, mask_BxS2_bf0)
    x, ctx_1024, mask_BxS2_bf0 = _rec_inputs()

    def _L0_attn_setup():
        import jax, jax.numpy as jnp
        import numpy as np
        B_, L_, D_MODEL = (4, 512, 256)
        D_INNER, D_STATE, D_CONV, DT_RANK = (512, 64, 4, 64)

        def _rmsnorm(x, w):
            eps = jnp.finfo(x.dtype).eps
            var = jnp.mean(jnp.square(x), axis=-1, keepdims=True)
            return x * jax.lax.rsqrt(var + eps) * w

        def _selective_scan(u, delta, A, Bm, Cm, Dp):
            du = jnp.swapaxes(delta, 0, 1)
            uu = jnp.swapaxes(u, 0, 1)
            Bu = jnp.swapaxes(Bm, 0, 1)
            Cu = jnp.swapaxes(Cm, 0, 1)

            def step(h, inp):
                d_t, u_t, B_t, C_t = inp
                dA = jnp.exp(d_t[..., None] * A)
                dBu = (d_t * u_t)[..., None] * B_t[:, None, :]
                h = dA * h + dBu
                y = jnp.einsum('bdn,bn->bd', h, C_t)
                return (h, y)
            h0 = jnp.zeros((u.shape[0], u.shape[2], A.shape[1]), u.dtype)
            _, ys = jax.lax.scan(step, h0, (du, uu, Bu, Cu))
            return jnp.swapaxes(ys, 0, 1) + u * Dp
        key = jax.random.key(seed)
        ks = jax.random.split(key, 8)
        s = 0.02
        x = jax.random.normal(ks[0], (B_, L_, D_MODEL), jnp.float32)
        W_in = jax.random.normal(ks[1], (2 * D_INNER, D_MODEL), jnp.float32) * s
        conv_w = jax.random.normal(ks[2], (D_INNER, 1, D_CONV), jnp.float32) * s
        conv_b = jnp.zeros((D_INNER,), jnp.float32)
        W_x = jax.random.normal(ks[3], (DT_RANK + 2 * D_STATE, D_INNER), jnp.float32) * s
        W_dt = jax.random.normal(ks[4], (D_INNER, DT_RANK), jnp.float32) * s
        b_dt = jax.random.uniform(ks[5], (D_INNER,), jnp.float32, minval=-4.6, maxval=-2.3)
        A_log = jnp.log(jnp.tile(jnp.arange(1, D_STATE + 1, dtype=jnp.float32), (D_INNER, 1)))
        Dp = jnp.ones((D_INNER,), jnp.float32)
        W_out = jax.random.normal(ks[6], (D_MODEL, D_INNER), jnp.float32) * s
        norm_w = jnp.ones((D_MODEL,), jnp.float32)
        return dict(x=x, norm_w=norm_w, W_in=W_in, conv_w=conv_w, conv_b=conv_b, W_x=W_x, W_dt=W_dt, b_dt=b_dt, A_log=A_log, Dp=Dp, W_out=W_out)
    _L0_attn_all = _L0_attn_setup()
    _L0_attn_in = {k: v for k, v in _L0_attn_all.items() if k in ('norm_w', 'W_in', 'conv_w', 'conv_b', 'W_x', 'W_dt', 'b_dt', 'A_log', 'Dp', 'W_out')}
    del _L0_attn_all

    def _L0_xattn_setup():
        import jax, jax.numpy as jnp
        import numpy as np
        D_MODEL = 256
        NUM_HEADS = 16
        D_K = D_MODEL // NUM_HEADS

        def _split_heads(x):
            B, S, _ = x.shape
            return x.reshape(B, S, NUM_HEADS, D_K).transpose(0, 2, 1, 3)
        key = jax.random.key(seed)
        k1, k2, k3, kq, kk, kv, ko = jax.random.split(key, 7)
        B, S = (4, 512)
        scale = 1.0 / np.sqrt(D_MODEL)
        return {'Q_in': jax.random.normal(k1, (B, S, D_MODEL), dtype=jnp.float32), 'K_in': jax.random.normal(k2, (B, S, D_MODEL), dtype=jnp.float32), 'V_in': jax.random.normal(k3, (B, S, D_MODEL), dtype=jnp.float32), 'W_q': jax.random.normal(kq, (D_MODEL, D_MODEL), dtype=jnp.float32) * scale, 'W_k': jax.random.normal(kk, (D_MODEL, D_MODEL), dtype=jnp.float32) * scale, 'W_v': jax.random.normal(kv, (D_MODEL, D_MODEL), dtype=jnp.float32) * scale, 'W_o': jax.random.normal(ko, (D_MODEL, D_MODEL), dtype=jnp.float32) * scale}
    _L0_xattn_all = _L0_xattn_setup()
    _L0_xattn_in = {k: v for k, v in _L0_xattn_all.items() if k in ('W_q', 'W_k', 'W_v', 'W_o')}
    del _L0_xattn_all

    def _L0_ffn_setup():
        import jax, jax.numpy as jnp
        import numpy as np
        EPS = 1e-05

        def _layernorm(x, w, b):
            mu = jnp.mean(x, axis=-1, keepdims=True)
            var = jnp.mean((x - mu) ** 2, axis=-1, keepdims=True)
            return (x - mu) * jax.lax.rsqrt(var + EPS) * w + b

        def _rope_tables(T, D, base=10000.0):
            inv_freq = 1.0 / base ** (jnp.arange(0, D, 2, dtype=jnp.float32) / D)
            t = jnp.arange(T, dtype=jnp.float32)
            freqs = jnp.einsum('i,j->ij', t, inv_freq)
            emb = jnp.concatenate([freqs, freqs], axis=-1)
            return (jnp.cos(emb), jnp.sin(emb))

        def _rotate_half(x):
            x1, x2 = (x[..., :x.shape[-1] // 2], x[..., x.shape[-1] // 2:])
            return jnp.concatenate([-x2, x1], axis=-1)

        def _attn(x, ln_w, ln_b, conv_w, attn_w, proj_w, n_head):
            B, T, C = x.shape
            D = C // n_head
            h = _layernorm(x, ln_w, ln_b)
            hc = jnp.transpose(h, (0, 2, 1))
            hc = jnp.pad(hc, ((0, 0), (0, 0), (2, 0)))
            hc = jax.lax.conv_general_dilated(hc, conv_w, window_strides=(1,), padding='VALID', dimension_numbers=('NCH', 'OIH', 'NCH'), feature_group_count=C)
            h = jnp.transpose(hc, (0, 2, 1))
            qkv = h @ attn_w
            q, k, v = jnp.split(qkv, 3, axis=-1)
            q = q.reshape(B, T, n_head, D)
            k = k.reshape(B, T, n_head, D)
            v = v.reshape(B, T, n_head, D)
            cos, sin = _rope_tables(T, D)
            cos = cos[None, :, None, :]
            sin = sin[None, :, None, :]
            q = q * cos + _rotate_half(q) * sin
            k = k * cos + _rotate_half(k) * sin
            scores = jnp.einsum('bqhd,bkhd->bhqk', q, k) / jnp.sqrt(jnp.float32(D))
            causal = jnp.tril(jnp.ones((T, T), dtype=bool))
            scores = jnp.where(causal, scores, jnp.float32(-1e+30))
            p = jax.nn.softmax(scores, axis=-1)
            y = jnp.einsum('bhqk,bkhd->bqhd', p, v).reshape(B, T, C)
            return y @ proj_w

        def _moe(x, ln_w, ln_b, router_w, expert_wv, expert_proj):
            h = _layernorm(x, ln_w, ln_b)
            logits = h @ router_w
            expert_idx = jnp.argmax(logits, axis=-1)
            E = router_w.shape[-1]
            out = jnp.zeros_like(x)
            for e in range(E):
                gv = h @ expert_wv[e]
                gate_raw, value = jnp.split(gv, 2, axis=-1)
                y = gate_raw * jax.nn.sigmoid(gate_raw) * value @ expert_proj[e]
                out = out + jnp.where((expert_idx == e)[..., None], y, 0.0)
            return out
        C, H, E, B, T = (256, 16, 4, 4, 256)
        Dff = 4 * C
        key = jax.random.key(seed)
        ks = jax.random.split(key, 8)
        s = 0.02
        return {'x': jax.random.normal(ks[0], (B, T, C), dtype=jnp.float32), 'ln1_w': jnp.ones((C,), jnp.float32), 'ln1_b': jnp.zeros((C,), jnp.float32), 'ln2_w': jnp.ones((C,), jnp.float32), 'ln2_b': jnp.zeros((C,), jnp.float32), 'conv_w': jax.random.normal(ks[1], (C, 1, 3), dtype=jnp.float32) * 0.1, 'attn_w': jax.random.normal(ks[2], (C, 3 * C), dtype=jnp.float32) * s, 'proj_w': jax.random.normal(ks[3], (C, C), dtype=jnp.float32) * s, 'router_w': jax.random.normal(ks[4], (C, E), dtype=jnp.float32) * s, 'expert_wv': jax.random.normal(ks[5], (E, C, 2 * Dff), dtype=jnp.float32) * s, 'expert_proj': jax.random.normal(ks[6], (E, Dff, C), dtype=jnp.float32) * s}
    _L0_ffn_all = _L0_ffn_setup()
    _L0_ffn_in = {k: v for k, v in _L0_ffn_all.items() if k in ('ln1_w', 'ln1_b', 'ln2_w', 'ln2_b', 'conv_w', 'attn_w', 'proj_w', 'router_w', 'expert_wv', 'expert_proj')}
    del _L0_ffn_all

    def _L1_attn_setup():
        import jax, jax.numpy as jnp
        import numpy as np
        HEADS = 16
        key = jax.random.key(seed)
        k1, k2, k3 = jax.random.split(key, 3)
        B, N, C = (4, 1024, 256)
        x = jax.random.normal(k1, (B, N, C), dtype=jnp.float32)
        w_qkv = jax.random.normal(k2, (3 * C, C), dtype=jnp.float32) * C ** (-0.5)
        w_proj = jax.random.normal(k3, (C, C), dtype=jnp.float32) * C ** (-0.5)
        b_proj = jnp.zeros((C,), dtype=jnp.float32)
        return {'x': x, 'w_qkv': w_qkv, 'w_proj': w_proj, 'b_proj': b_proj}
    _L1_attn_all = _L1_attn_setup()
    _L1_attn_in = {k: v for k, v in _L1_attn_all.items() if k in ('w_qkv', 'w_proj', 'b_proj')}
    del _L1_attn_all

    def _L1_xattn_setup():
        import jax, jax.numpy as jnp
        import numpy as np
        B, LX, LY, D = (32, 256, 128, 256)
        key = jax.random.key(seed)
        k1, k2, k3, k4 = jax.random.split(key, 4)
        x = jax.random.normal(k1, (B, LX, D), dtype=jnp.float32)
        y = jax.random.normal(k2, (B, LY, D), dtype=jnp.float32)
        y_mask = jnp.zeros((B, LY), dtype=bool)
        W = jax.random.normal(k3, (D, D), dtype=jnp.float32) * (1.0 / np.sqrt(D))
        b = jax.random.normal(k4, (D,), dtype=jnp.float32) * 0.01
        return {'x': x, 'y': y, 'y_mask': y_mask, 'W': W, 'b': b}
    _L1_xattn_all = _L1_xattn_setup()
    _L1_xattn_in = {k: v for k, v in _L1_xattn_all.items() if k in ('W', 'b')}
    del _L1_xattn_all

    def _L1_ffn_setup():
        import jax, jax.numpy as jnp
        import numpy as np
        EMB = 256
        FF = 4 * EMB

        def _ternary(w):
            scale = jnp.maximum(jnp.mean(jnp.abs(w)), 1e-08)
            w_t = jnp.clip(jnp.round(w / scale), -1.0, 1.0)
            return w + jax.lax.stop_gradient(w_t - w)
        key = jax.random.key(seed)
        kx, k1, k2, kb1, kb2 = jax.random.split(key, 5)
        x = jax.random.normal(kx, (4, 512, EMB), dtype=jnp.float32)
        lim1 = 1.0 / np.sqrt(EMB)
        lim2 = 1.0 / np.sqrt(FF)
        W1 = jax.random.uniform(k1, (FF, EMB), jnp.float32, -lim1, lim1)
        b1 = jax.random.uniform(kb1, (FF,), jnp.float32, -lim1, lim1)
        W2 = jax.random.uniform(k2, (EMB, FF), jnp.float32, -lim2, lim2)
        b2 = jax.random.uniform(kb2, (EMB,), jnp.float32, -lim2, lim2)
        return {'x': x, 'W1': W1, 'b1': b1, 'W2': W2, 'b2': b2}
    _L1_ffn_all = _L1_ffn_setup()
    _L1_ffn_in = {k: v for k, v in _L1_ffn_all.items() if k in ('W1', 'b1', 'W2', 'b2')}
    del _L1_ffn_all
    return {'x': x, 'ctx_1024': ctx_1024, 'mask_BxS2_bf0': mask_BxS2_bf0, 'L0_attn_norm_w': _L0_attn_in['norm_w'], 'L0_attn_W_in': _L0_attn_in['W_in'], 'L0_attn_conv_w': _L0_attn_in['conv_w'], 'L0_attn_conv_b': _L0_attn_in['conv_b'], 'L0_attn_W_x': _L0_attn_in['W_x'], 'L0_attn_W_dt': _L0_attn_in['W_dt'], 'L0_attn_b_dt': _L0_attn_in['b_dt'], 'L0_attn_A_log': _L0_attn_in['A_log'], 'L0_attn_Dp': _L0_attn_in['Dp'], 'L0_attn_W_out': _L0_attn_in['W_out'], 'L0_xattn_W_q': _L0_xattn_in['W_q'], 'L0_xattn_W_k': _L0_xattn_in['W_k'], 'L0_xattn_W_v': _L0_xattn_in['W_v'], 'L0_xattn_W_o': _L0_xattn_in['W_o'], 'L0_ffn_ln1_w': _L0_ffn_in['ln1_w'], 'L0_ffn_ln1_b': _L0_ffn_in['ln1_b'], 'L0_ffn_ln2_w': _L0_ffn_in['ln2_w'], 'L0_ffn_ln2_b': _L0_ffn_in['ln2_b'], 'L0_ffn_conv_w': _L0_ffn_in['conv_w'], 'L0_ffn_attn_w': _L0_ffn_in['attn_w'], 'L0_ffn_proj_w': _L0_ffn_in['proj_w'], 'L0_ffn_router_w': _L0_ffn_in['router_w'], 'L0_ffn_expert_wv': _L0_ffn_in['expert_wv'], 'L0_ffn_expert_proj': _L0_ffn_in['expert_proj'], 'L1_attn_w_qkv': _L1_attn_in['w_qkv'], 'L1_attn_w_proj': _L1_attn_in['w_proj'], 'L1_attn_b_proj': _L1_attn_in['b_proj'], 'L1_xattn_W': _L1_xattn_in['W'], 'L1_xattn_b': _L1_xattn_in['b'], 'L1_ffn_W1': _L1_ffn_in['W1'], 'L1_ffn_b1': _L1_ffn_in['b1'], 'L1_ffn_W2': _L1_ffn_in['W2'], 'L1_ffn_b2': _L1_ffn_in['b2']}

def reference(x, ctx_1024, mask_BxS2_bf0, L0_attn_norm_w, L0_attn_W_in, L0_attn_conv_w, L0_attn_conv_b, L0_attn_W_x, L0_attn_W_dt, L0_attn_b_dt, L0_attn_A_log, L0_attn_Dp, L0_attn_W_out, L0_xattn_W_q, L0_xattn_W_k, L0_xattn_W_v, L0_xattn_W_o, L0_ffn_ln1_w, L0_ffn_ln1_b, L0_ffn_ln2_w, L0_ffn_ln2_b, L0_ffn_conv_w, L0_ffn_attn_w, L0_ffn_proj_w, L0_ffn_router_w, L0_ffn_expert_wv, L0_ffn_expert_proj, L1_attn_w_qkv, L1_attn_w_proj, L1_attn_b_proj, L1_xattn_W, L1_xattn_b, L1_ffn_W1, L1_ffn_b1, L1_ffn_W2, L1_ffn_b2):
    import jax
    import jax.numpy as jnp

    def _L0_attn_ref(x, norm_w, W_in, conv_w, conv_b, W_x, W_dt, b_dt, A_log, Dp, W_out):
        import jax, jax.numpy as jnp
        import numpy as np
        B_, L_, D_MODEL = (4, 512, 256)
        D_INNER, D_STATE, D_CONV, DT_RANK = (512, 64, 4, 64)

        def _rmsnorm(x, w):
            eps = jnp.finfo(x.dtype).eps
            var = jnp.mean(jnp.square(x), axis=-1, keepdims=True)
            return x * jax.lax.rsqrt(var + eps) * w

        def _selective_scan(u, delta, A, Bm, Cm, Dp):
            du = jnp.swapaxes(delta, 0, 1)
            uu = jnp.swapaxes(u, 0, 1)
            Bu = jnp.swapaxes(Bm, 0, 1)
            Cu = jnp.swapaxes(Cm, 0, 1)

            def step(h, inp):
                d_t, u_t, B_t, C_t = inp
                dA = jnp.exp(d_t[..., None] * A)
                dBu = (d_t * u_t)[..., None] * B_t[:, None, :]
                h = dA * h + dBu
                y = jnp.einsum('bdn,bn->bd', h, C_t)
                return (h, y)
            h0 = jnp.zeros((u.shape[0], u.shape[2], A.shape[1]), u.dtype)
            _, ys = jax.lax.scan(step, h0, (du, uu, Bu, Cu))
            return jnp.swapaxes(ys, 0, 1) + u * Dp
        xn = _rmsnorm(x, norm_w)
        xz = xn @ W_in.T
        xm, z = jnp.split(xz, 2, axis=-1)
        xc = jnp.swapaxes(xm, 1, 2)
        xc = jax.lax.conv_general_dilated(xc, conv_w, window_strides=(1,), padding=[(D_CONV - 1, 0)], feature_group_count=D_INNER, dimension_numbers=('NCH', 'OIH', 'NCH'))
        xc = jax.nn.silu(xc + conv_b[None, :, None])
        u = jnp.swapaxes(xc, 1, 2)
        x_dbl = u @ W_x.T
        dt, Bm, Cm = jnp.split(x_dbl, [DT_RANK, DT_RANK + D_STATE], axis=-1)
        delta = jax.nn.softplus(dt @ W_dt.T + b_dt)
        A = -jnp.exp(A_log)
        y = _selective_scan(u, delta, A, Bm, Cm, Dp)
        y = y * jax.nn.silu(z)
        out = y @ W_out.T
        return out + x

    def _L0_xattn_ref(Q_in, K_in, V_in, W_q, W_k, W_v, W_o):
        import jax, jax.numpy as jnp
        import numpy as np
        D_MODEL = 256
        NUM_HEADS = 16
        D_K = D_MODEL // NUM_HEADS

        def _split_heads(x):
            B, S, _ = x.shape
            return x.reshape(B, S, NUM_HEADS, D_K).transpose(0, 2, 1, 3)
        Q = _split_heads(Q_in @ W_q.T)
        K = _split_heads(K_in @ W_k.T)
        V = _split_heads(V_in @ W_v.T)
        scores = jnp.einsum('bhqd,bhkd->bhqk', Q, K) / jnp.sqrt(jnp.float32(D_K))
        attn = jax.nn.softmax(scores, axis=-1)
        out = jnp.einsum('bhqk,bhkd->bhqd', attn, V)
        B, H, S, dk = out.shape
        concat = out.transpose(0, 2, 1, 3).reshape(B, S, H * dk)
        return concat @ W_o.T

    def _L0_ffn_ref(x, ln1_w, ln1_b, ln2_w, ln2_b, conv_w, attn_w, proj_w, router_w, expert_wv, expert_proj):
        import jax, jax.numpy as jnp
        import numpy as np
        EPS = 1e-05

        def _layernorm(x, w, b):
            mu = jnp.mean(x, axis=-1, keepdims=True)
            var = jnp.mean((x - mu) ** 2, axis=-1, keepdims=True)
            return (x - mu) * jax.lax.rsqrt(var + EPS) * w + b

        def _rope_tables(T, D, base=10000.0):
            inv_freq = 1.0 / base ** (jnp.arange(0, D, 2, dtype=jnp.float32) / D)
            t = jnp.arange(T, dtype=jnp.float32)
            freqs = jnp.einsum('i,j->ij', t, inv_freq)
            emb = jnp.concatenate([freqs, freqs], axis=-1)
            return (jnp.cos(emb), jnp.sin(emb))

        def _rotate_half(x):
            x1, x2 = (x[..., :x.shape[-1] // 2], x[..., x.shape[-1] // 2:])
            return jnp.concatenate([-x2, x1], axis=-1)

        def _attn(x, ln_w, ln_b, conv_w, attn_w, proj_w, n_head):
            B, T, C = x.shape
            D = C // n_head
            h = _layernorm(x, ln_w, ln_b)
            hc = jnp.transpose(h, (0, 2, 1))
            hc = jnp.pad(hc, ((0, 0), (0, 0), (2, 0)))
            hc = jax.lax.conv_general_dilated(hc, conv_w, window_strides=(1,), padding='VALID', dimension_numbers=('NCH', 'OIH', 'NCH'), feature_group_count=C)
            h = jnp.transpose(hc, (0, 2, 1))
            qkv = h @ attn_w
            q, k, v = jnp.split(qkv, 3, axis=-1)
            q = q.reshape(B, T, n_head, D)
            k = k.reshape(B, T, n_head, D)
            v = v.reshape(B, T, n_head, D)
            cos, sin = _rope_tables(T, D)
            cos = cos[None, :, None, :]
            sin = sin[None, :, None, :]
            q = q * cos + _rotate_half(q) * sin
            k = k * cos + _rotate_half(k) * sin
            scores = jnp.einsum('bqhd,bkhd->bhqk', q, k) / jnp.sqrt(jnp.float32(D))
            causal = jnp.tril(jnp.ones((T, T), dtype=bool))
            scores = jnp.where(causal, scores, jnp.float32(-1e+30))
            p = jax.nn.softmax(scores, axis=-1)
            y = jnp.einsum('bhqk,bkhd->bqhd', p, v).reshape(B, T, C)
            return y @ proj_w

        def _moe(x, ln_w, ln_b, router_w, expert_wv, expert_proj):
            h = _layernorm(x, ln_w, ln_b)
            logits = h @ router_w
            expert_idx = jnp.argmax(logits, axis=-1)
            E = router_w.shape[-1]
            out = jnp.zeros_like(x)
            for e in range(E):
                gv = h @ expert_wv[e]
                gate_raw, value = jnp.split(gv, 2, axis=-1)
                y = gate_raw * jax.nn.sigmoid(gate_raw) * value @ expert_proj[e]
                out = out + jnp.where((expert_idx == e)[..., None], y, 0.0)
            return out
        n_head = 16
        x = x + _attn(x, ln1_w, ln1_b, conv_w, attn_w, proj_w, n_head)
        x = x + _moe(x, ln2_w, ln2_b, router_w, expert_wv, expert_proj)
        return x

    def _L1_attn_ref(x, w_qkv, w_proj, b_proj):
        import jax, jax.numpy as jnp
        import numpy as np
        HEADS = 16
        B, N, C = x.shape
        H = HEADS
        D = C // H
        qkv = x @ w_qkv.T
        q, k, v = jnp.split(qkv, 3, axis=-1)

        def to_bhdn(t):
            return t.reshape(B, N, H, D).transpose(0, 2, 3, 1)
        q = jax.nn.relu(to_bhdn(q))
        k = jax.nn.relu(to_bhdn(k))
        v = to_bhdn(v)
        eps = jnp.finfo(q.dtype).eps
        ksum = k.sum(axis=-1)
        z = 1.0 / (jnp.einsum('bhd,bhdn->bhn', ksum, q) + eps)
        context = jnp.einsum('bhdn,bhen->bhde', v, k)
        out = jnp.einsum('bhde,bhen->bhdn', context, q)
        out = out * z[:, :, None, :]
        out = out.transpose(0, 3, 1, 2).reshape(B, N, C)
        return out @ w_proj.T + b_proj

    def _L1_xattn_ref(x, y, y_mask, W, b):
        import jax, jax.numpy as jnp
        import numpy as np
        B, LX, LY, D = (32, 256, 128, 256)
        x_proj = jax.nn.relu(jnp.einsum('bxd,ed->bxe', x, W) + b)
        y_proj = jax.nn.relu(jnp.einsum('byd,ed->bye', y, W) + b)
        scores = jnp.einsum('bxd,byd->bxy', x_proj, y_proj)
        scores = jnp.where(y_mask[:, None, :], -jnp.inf, scores)
        att = jax.nn.softmax(scores, axis=-1)
        return jnp.einsum('bxy,byd->bxd', att, y)

    def _L1_ffn_ref(x, W1, b1, W2, b2):
        import jax, jax.numpy as jnp
        import numpy as np
        EMB = 256
        FF = 4 * EMB

        def _ternary(w):
            scale = jnp.maximum(jnp.mean(jnp.abs(w)), 1e-08)
            w_t = jnp.clip(jnp.round(w / scale), -1.0, 1.0)
            return w + jax.lax.stop_gradient(w_t - w)
        h = jnp.einsum('bsd,fd->bsf', x, _ternary(W1)) + b1
        h = jax.nn.gelu(h, approximate=False)
        out = jnp.einsum('bsf,df->bsd', h, _ternary(W2)) + b2
        return out
    x = x + _L0_attn_ref(_layernorm(x, axis=-1), L0_attn_norm_w, L0_attn_W_in, L0_attn_conv_w, L0_attn_conv_b, L0_attn_W_x, L0_attn_W_dt, L0_attn_b_dt, L0_attn_A_log, L0_attn_Dp, L0_attn_W_out)
    x = x + _L0_xattn_ref(_layernorm(x, axis=-1), ctx_1024, ctx_1024, L0_xattn_W_q, L0_xattn_W_k, L0_xattn_W_v, L0_xattn_W_o)
    x = x + _L0_ffn_ref(_layernorm(x, axis=-1), L0_ffn_ln1_w, L0_ffn_ln1_b, L0_ffn_ln2_w, L0_ffn_ln2_b, L0_ffn_conv_w, L0_ffn_attn_w, L0_ffn_proj_w, L0_ffn_router_w, L0_ffn_expert_wv, L0_ffn_expert_proj)
    x = x + _L1_attn_ref(_layernorm(x, axis=-1), L1_attn_w_qkv, L1_attn_w_proj, L1_attn_b_proj)
    x = x + _L1_xattn_ref(_layernorm(x, axis=-1), ctx_1024, mask_BxS2_bf0, L1_xattn_W, L1_xattn_b)
    x = x + _L1_ffn_ref(_layernorm(x, axis=-1), L1_ffn_W1, L1_ffn_b1, L1_ffn_W2, L1_ffn_b2)
    return x

_drawn_inputs = setup_inputs


def setup_inputs(seed=0):
    import zlib

    import numpy as np

    out = dict(_drawn_inputs(seed))
    spreads = {'L0_attn_norm_w': (1.0, 0.6),
     'L0_attn_conv_b': (0.0, 0.8),
     'L0_attn_Dp': (1.0, 0.6),
     'L0_ffn_ln1_w': (1.0, 0.6),
     'L0_ffn_ln1_b': (0.0, 0.8),
     'L0_ffn_ln2_w': (1.0, 0.6),
     'L0_ffn_ln2_b': (0.0, 0.8),
     'L1_attn_b_proj': (0.0, 0.8)}
    factors = {'L0_attn_W_in': 8.0,
     'L0_attn_conv_w': 8.0,
     'L0_attn_W_x': 8.0,
     'L0_attn_W_dt': 8.0,
     'L0_attn_b_dt': 8.0,
     'L0_attn_A_log': 8.0,
     'L0_attn_W_out': 8.0,
     'L0_ffn_conv_w': 8.0,
     'L0_ffn_attn_w': 8.0,
     'L0_ffn_proj_w': 8.0,
     'L0_ffn_router_w': 4.622,
     'L0_ffn_expert_wv': 3.992,
     'L0_ffn_expert_proj': 3.978,
     'L1_xattn_b': 34.065,
     'L1_ffn_b1': 23.365,
     'L1_ffn_b2': 64.0,
     'L1_attn_w_qkv': 2.911,
     'L1_attn_w_proj': 2.958}
    for name, (base, spread) in spreads.items():
        noise = np.random.default_rng([zlib.crc32(name.encode()), seed]).standard_normal(out[name].shape)
        drawn = base * np.exp(spread * noise) if base else spread * noise
        out[name] = jnp.asarray(drawn.astype(out[name].dtype))
    for name, factor in factors.items():
        out[name] = (out[name] * factor).astype(out[name].dtype)
    return out
```

```python
from contextlib import ExitStack

import concourse.bass as bass
from concourse import mybir

F32 = mybir.dt.float32
BF16 = mybir.dt.bfloat16
I32 = mybir.dt.int32
ALU = mybir.AluOpType
ACT = mybir.ActivationFunctionType
AX = mybir.AxisListType

P = 128
B, T, D = 2, 1024, 256
N = B * T
C = D // P
W = 512
NCH = N // W
CPB = T // W
DI, DS, DC, DR = 512, 64, 4, 64
CI = DI // P
H, DK = 16, 16
S2 = 77
E_, FF = 4, 1024
TAPS = 3
SLOTS = 8
EPS = 1e-5
EPS_F32 = 1.1920929e-07
NEG = -1e30


class Signal:

    def __init__(self, sem):
        self.sem, self.base = sem, 0

    def at(self, k):
        return self.base + k

    def passed(self, k):
        self.base += k


class Core:

    def __init__(self, nc, ctx):
        self.nc, self.ctx, self.signals, self.names = nc, ctx, {}, 0

    def sb(self, name, shape, dt=F32, ctx=None):
        self.names += 1
        return (ctx or self.ctx).enter_context(self.nc.sbuf_tensor(f"{name}_{self.names}", shape, dt))

    def sig(self, name):
        if name not in self.signals:
            self.signals[name] = Signal(self.ctx.enter_context(self.nc.semaphore(name)))
        return self.signals[name]


def spread(ap, k):
    p, n = ap.shape
    return ap.rearrange("p (a n) -> p a n", a=1).broadcast_to([p, k, n])


def load(k, pairs):
    moved = k.sig("moved")
    with k.nc.Block() as block:
        @block.sync
        def _(sp):
            for dst, src in pairs:
                sp.dma_start(dst, src).then_inc(moved.sem, 16)
            sp.wait_ge(moved.sem, moved.at(16 * len(pairs)))
    moved.passed(16 * len(pairs))


def norm(k, src, dst, centre=True, eps=EPS, weight=None, bias=None, ctx_name="n"):
    nc, ps = k.nc, k.ps
    mean_ready, centred, squared = k.sig("mean_ready"), k.sig("centred"), k.sig("squared")
    var_ready, root_ready, root_squared = k.sig("var_ready"), k.sig("root_ready"), k.sig("root_squared")
    newton, corrected, rstd_ready = k.sig("newton"), k.sig("corrected"), k.sig("rstd_ready")
    scaled, normed = k.sig("scaled"), k.sig("normed")
    affine = weight is not None
    with ExitStack() as ctx:
        sq = k.sb("norm_sq", [P, 2, C, W], ctx=ctx)
        r0 = k.sb("norm_r0", [P, 2, W], ctx=ctx)
        r0sq = k.sb("norm_r0sq", [P, 2, W], ctx=ctx)
        rstd = k.sb("norm_rstd", [P, 2, W], ctx=ctx)
        block = ctx.enter_context(nc.Block())

        def chunk(t, c):
            return t[:, :, c * W:(c + 1) * W]

        at = chunk(src, 0) if not centre else None
        body = dst if centre else src

        @block.tensor
        def _(pe):
            def mean(c):
                if c >= 2:
                    pe.wait_ge(centred.sem, centred.at(c - 1))
                for b in range(C):
                    mm = pe.matmul(ps[:, c % 2, :], k.inv[:, :], src[:, b, c * W:(c + 1) * W],
                                   start=(b == 0), stop=(b == C - 1))
                mm.then_inc(mean_ready.sem, 1)

            def var(c):
                pe.wait_ge(squared.sem, squared.at(c + 1))
                if c >= 2:
                    pe.wait_ge(newton.sem, newton.at(c - 1))
                for b in range(C):
                    mm = pe.matmul(ps[:, 2 + c % 2, :], k.inv[:, :], sq[:, c % 2, b, :],
                                   start=(b == 0), stop=(b == C - 1))
                mm.then_inc(var_ready.sem, 1)

            if centre:
                mean(0)
            for c in range(NCH):
                if centre and c + 1 < NCH:
                    mean(c + 1)
                var(c)

        @block.vector
        def _(dve):
            def centre_chunk(c):
                dve.wait_ge(mean_ready.sem, mean_ready.at(c + 1))
                dve.tensor_tensor(chunk(dst, c), chunk(src, c), spread(ps[:, c % 2, :], C),
                                  ALU.subtract).then_inc(centred.sem, 1)

            if centre:
                centre_chunk(0)
            for c in range(NCH):
                if centre and c + 1 < NCH:
                    centre_chunk(c + 1)
                dve.wait_ge(var_ready.sem, var_ready.at(c + 1))
                dve.wait_ge(root_squared.sem, root_squared.at(c + 1))
                if c >= 2:
                    dve.wait_ge(scaled.sem, scaled.at(c - 1))
                dve.scalar_tensor_tensor(rstd[:, c % 2, :], ps[:, 2 + c % 2, :], float(eps), r0sq[:, c % 2, :],
                                         ALU.add, ALU.mult).then_inc(newton.sem, 1)
                dve.wait_ge(newton.sem, newton.at(c + 1))
                dve.tensor_scalar(rstd[:, c % 2, :], rstd[:, c % 2, :], -0.5, 1.5, ALU.mult,
                                  ALU.add).then_inc(corrected.sem, 1)
                dve.wait_ge(corrected.sem, corrected.at(c + 1))
                dve.tensor_tensor(rstd[:, c % 2, :], rstd[:, c % 2, :], r0[:, c % 2, :],
                                  ALU.mult).then_inc(rstd_ready.sem, 1)

        @block.scalar
        def _(act):
            def square(c):
                if centre:
                    act.wait_ge(centred.sem, centred.at(c + 1))
                if c >= 2:
                    act.wait_ge(var_ready.sem, var_ready.at(c - 1))
                act.activation(sq[:, c % 2, :, :], chunk(body, c), ACT.Square).then_inc(squared.sem, 1)

            def affine_chunk(c):
                act.wait_ge(scaled.sem, scaled.at(c + 1))
                for b in range(C):
                    x = dst[:, b, c * W:(c + 1) * W]
                    act.activation(x, x, ACT.Identity, scale=weight[:, b:b + 1],
                                   bias=bias[:, b:b + 1] if bias is not None else 0.0).then_inc(normed.sem, 1)

            square(0)
            for c in range(NCH):
                if c + 1 < NCH:
                    square(c + 1)
                act.wait_ge(var_ready.sem, var_ready.at(c + 1))
                if c >= 2:
                    act.wait_ge(rstd_ready.sem, rstd_ready.at(c - 1))
                act.activation(r0[:, c % 2, :], ps[:, 2 + c % 2, :], ACT.Abs_reciprocal_sqrt,
                               bias=k.eps[:, 0:1] if eps == EPS else k.eps[:, 1:2]).then_inc(root_ready.sem, 1)
                act.wait_ge(root_ready.sem, root_ready.at(c + 1))
                act.activation(r0sq[:, c % 2, :], r0[:, c % 2, :], ACT.Square).then_inc(root_squared.sem, 1)
                if affine and c >= 1:
                    affine_chunk(c - 1)
            if affine:
                affine_chunk(NCH - 1)

        @block.gpsimd
        def _(pool):
            for c in range(NCH):
                pool.wait_ge(rstd_ready.sem, rstd_ready.at(c + 1))
                if not centre:
                    pool.wait_ge(squared.sem, squared.at(c + 1))
                pool.tensor_tensor(chunk(dst, c), chunk(body, c), spread(rstd[:, c % 2, :], C),
                                   ALU.mult).then_inc(scaled.sem, 1)
            pool.wait_ge(scaled.sem, scaled.at(NCH))

        ctx.pop_all().close()
    if centre:
        mean_ready.passed(NCH)
        centred.passed(NCH)
    for s in (squared, var_ready, root_ready, root_squared, newton, corrected, rstd_ready, scaled):
        s.passed(NCH)
    if affine:
        normed.passed(NCH * C)


class Tile:

    def __init__(self, products, engine, take, rows=P, cols=W):
        self.products, self.engine, self.take, self.rows, self.cols = products, engine, take, rows, cols


def project(k, tiles, banks=8):
    nc, ps = k.nc, k.ps
    summed = k.sig("summed")
    taken = {"act": k.sig("taken_act"), "dve": k.sig("taken_dve")}
    done = {"act": 0, "dve": 0}
    count = []
    for t in tiles:
        done[t.engine] += 1
        count.append(done[t.engine])
    with nc.Block() as block:
        @block.tensor
        def _(pe):
            for n, t in enumerate(tiles):
                if n >= banks:
                    old = tiles[n - banks]
                    pe.wait_ge(taken[old.engine].sem, taken[old.engine].at(count[n - banks]))
                for i, (lhs, rhs) in enumerate(t.products):
                    mm = pe.matmul(ps[0:t.rows, n % banks, 0:t.cols], lhs, rhs, start=(i == 0),
                                   stop=(i == len(t.products) - 1))
                mm.then_inc(summed.sem, 1)

        def take_all(eng, name):
            for n, t in enumerate(tiles):
                if t.engine == name:
                    eng.wait_ge(summed.sem, summed.at(n + 1))
                    t.take(eng, ps[0:t.rows, n % banks, 0:t.cols]).then_inc(taken[name].sem, 1)

        @block.scalar
        def _(act):
            take_all(act, "act")

        @block.vector
        def _(dve):
            take_all(dve, "dve")
    summed.passed(len(tiles))
    for name in taken:
        taken[name].passed(done[name])


def copy_to(dst, func=ACT.Copy, scale=1.0):
    return lambda eng, bank: eng.activation(dst, bank, func, scale=scale)


def dve_copy_to(dst):
    return lambda eng, bank: eng.tensor_copy(dst, bank)


def steps(k, name, ops):
    chain = k.sig(name)
    with k.nc.Block() as block:
        def run(eng, mine):
            for n, (who, call) in enumerate(ops):
                if who == mine:
                    if n:
                        eng.wait_ge(chain.sem, chain.at(n))
                    call(eng).then_inc(chain.sem, 1)
            eng.wait_ge(chain.sem, chain.at(len(ops)))

        @block.vector
        def _(dve):
            run(dve, "dve")

        @block.scalar
        def _(act):
            run(act, "act")

        @block.gpsimd
        def _(pool):
            run(pool, "pool")
    chain.passed(len(ops))


def add_into(k, x, y):
    added = k.sig("added")
    with k.nc.Block() as block:
        @block.vector
        def _(dve):
            dve.tensor_tensor(x[:, :, 0:N // 2], x[:, :, 0:N // 2], y[:, :, 0:N // 2], ALU.add)\
               .then_inc(added.sem, 1)
            dve.tensor_tensor(x[:, 0, N // 2:N], x[:, 0, N // 2:N], y[:, 0, N // 2:N], ALU.add)\
               .then_inc(added.sem, 1)
            dve.wait_ge(added.sem, added.at(3))

        @block.gpsimd
        def _(pool):
            pool.tensor_tensor(x[:, 1, N // 2:N], x[:, 1, N // 2:N], y[:, 1, N // 2:N], ALU.add)\
                .then_inc(added.sem, 1)
    added.passed(3)



def mamba(k, a):
    nc, ps, X = k.nc, k.ps, k.X
    with ExitStack() as ctx:
        XN = k.sb("XN", [P, C, N], ctx=ctx)
        norm(k, X, XN)
        add_into(k, X, XN)
        w_in = k.sb("w_in", [P, C, 2 * DI], ctx=ctx)
        w_x = k.sb("w_x", [P, CI, DR + DS + 2 * DS], ctx=ctx)
        w_dt = k.sb("w_dt", [DR, DI], ctx=ctx)
        w_out = k.sb("w_out", [P, CI, D], ctx=ctx)
        vec = k.sb("mamba_vec", [P, CI, DC + 3], ctx=ctx)
        A = k.sb("A", [P, CI, DS], ctx=ctx)
        rms_w = k.sb("rms_w", [P, C], ctx=ctx)
        load(k, [(w_in[:], a["w_in"]), (w_x[:], a["w_x"]), (w_dt[:], a["w_dt"]), (w_out[:], a["w_out"]),
                 (vec[:], a["mamba_vec"]), (A[:], a["a_log"]), (rms_w[:], a["rms_w"])])
        norm(k, XN, XN, centre=False, eps=EPS_F32, weight=rms_w)
        diag = k.sb("diag_skip", [P, CI, P], ctx=ctx)
        ops = [("act", lambda e: e.activation(A[:], A[:], ACT.Exp)),
               ("dve", lambda e: e.tensor_scalar(A[:], A[:], -1.0, None, ALU.mult))]
        for c in range(CI):
            ops.append(("dve", lambda e, c=c: e.tensor_scalar(diag[:, c, :], k.ident[:, :], vec[:, c, DC + 2:DC + 3],
                                                              None, ALU.mult)))
        steps(k, "chain", ops)
        for b in range(B):
            with ExitStack() as bctx:
                mamba_batch(k, a, b, XN, w_in, w_x, w_dt, w_out, vec, A, diag, bctx)


def mamba_batch(k, a, b, XN, w_in, w_x, w_dt, w_out, vec, A, diag, ctx):
    nc, ps, X = k.nc, k.ps, k.X
    zs = k.sb(f"zs{b}", [P, CI, T], ctx=ctx)
    u = k.sb(f"u{b}", [P, CI, T], ctx=ctx)
    delta = k.sb(f"delta{b}", [P, CI, T], ctx=ctx)
    du = k.sb(f"du{b}", [P, CI, T], ctx=ctx)
    c_hm = k.sb(f"c_hm{b}", [P, T], BF16, ctx=ctx)
    c_lo = k.sb(f"c_lo{b}", [DS, T], BF16, ctx=ctx)
    with ExitStack() as c2:
        xm = k.sb(f"xm{b}", [P, CI, DC - 1 + T], ctx=c2)
        tiles = []
        for h in range(CPB):
            for m in range(2 * CI):
                prods = [(w_in[:, c, m * P:(m + 1) * P], XN[:, c, b * T + h * W:b * T + (h + 1) * W]) for c in range(C)]
                if m < CI:
                    dst = xm[:, m, DC - 1 + h * W:DC - 1 + (h + 1) * W]
                    tiles.append(Tile(prods, "dve", dve_copy_to(dst)))
                else:
                    tiles.append(Tile(prods, "act", copy_to(zs[:, m - CI, h * W:(h + 1) * W], ACT.Silu)))
        project(k, tiles)
        ops = [("dve", lambda e: e.memset(xm[:, :, 0:DC - 1], 0.0))]
        for c in range(CI):
            ops.append(("dve", lambda e, c=c: e.tensor_scalar(u[:, c, :], xm[:, c, 0:T], vec[:, c, 0:1], None, ALU.mult)))
            for j in range(1, DC):
                ops.append(("dve", lambda e, c=c, j=j: e.scalar_tensor_tensor(
                    u[:, c, :], xm[:, c, j:j + T], vec[:, c, j:j + 1], u[:, c, :], ALU.mult, ALU.add)))
        for c in range(CI):
            ops.append(("act", lambda e, c=c: e.activation(u[:, c, :], u[:, c, :], ACT.Silu, bias=vec[:, c, DC:DC + 1])))
        steps(k, "chain", ops)
    with ExitStack() as c2:
        dt = k.sb(f"dt{b}", [DR, T], ctx=c2)
        bs = k.sb(f"bs{b}", [DS, T], ctx=c2)
        cs = k.sb(f"cs{b}", [P, T], ctx=c2)
        tiles = []
        for h in range(CPB):
            for dst, o, n in ((dt, 0, DR), (bs, DR, DS), (cs, DR + DS, 2 * DS)):
                prods = [(w_x[:, c, o:o + n], u[:, c, h * W:(h + 1) * W]) for c in range(CI)]
                tiles.append(Tile(prods, "act", copy_to(dst[:, h * W:(h + 1) * W]), rows=n))
        project(k, tiles)
        load(k, [(k.b_rows[b], bs[:])])
        tiles = []
        for h in range(CPB):
            for m in range(CI):
                tiles.append(Tile([(w_dt[:, m * P:(m + 1) * P], dt[:, h * W:(h + 1) * W])], "act",
                                  lambda e, bank, m=m, h=h: e.activation(delta[:, m, h * W:(h + 1) * W], bank,
                                                                         ACT.Identity, bias=vec[:, m, DC + 1:DC + 2])))
        project(k, tiles)
        hi = k.sb(f"c_hi{b}", [P, T], BF16, ctx=c2)
        steps(k, "chain", [
            ("dve", lambda e: e.tensor_copy(c_hm[:], cs[:])),
            ("dve", lambda e: e.tensor_tensor(cs[:], cs[:], c_hm[:], ALU.subtract)),
            ("dve", lambda e: e.tensor_copy(hi[:], cs[:])),
            ("dve", lambda e: e.tensor_copy(c_hm[DS:P, :], hi[DS:P, :])),
            ("dve", lambda e: e.tensor_tensor(cs[0:DS, :], cs[0:DS, :], hi[0:DS, :], ALU.subtract)),
            ("dve", lambda e: e.tensor_copy(c_lo[:], cs[0:DS, :])),
        ])
    with ExitStack() as c2:
        e_ = k.sb(f"sp_e{b}", [P, CI, T // 2], ctx=c2)
        s_ = k.sb(f"sp_s{b}", [P, CI, T // 2], ctx=c2)
        q_ = k.sb(f"sp_q{b}", [P, CI, T // 2], ctx=c2)
        for h in range(2):
            x = delta[:, :, h * (T // 2):(h + 1) * (T // 2)]
            ops = [("act", lambda e, x=x: e.activation(e_[:], x, ACT.Abs)),
                   ("act", lambda e: e.activation(e_[:], e_[:], ACT.Exp, scale=-1.0)),
                   ("dve", lambda e: e.tensor_scalar(s_[:], e_[:], 2.0, None, ALU.add)),
                   ("dve", lambda e: e.reciprocal(s_[:], s_[:])),
                   ("dve", lambda e: e.tensor_tensor(s_[:], s_[:], e_[:], ALU.mult)),
                   ("act", lambda e: e.activation(e_[:], s_[:], ACT.Square)),
                   ("dve", lambda e: e.tensor_scalar(q_[:], e_[:], 1.0 / 17, None, ALU.mult))]
            for n in (15, 13, 11, 9, 7, 5, 3):
                ops.append(("dve", lambda e, n=n: e.scalar_tensor_tensor(q_[:], q_[:], 1.0 / n, e_[:], ALU.add, ALU.mult)))
            ops += [("dve", lambda e: e.scalar_tensor_tensor(q_[:], q_[:], 1.0, s_[:], ALU.add, ALU.mult)),
                    ("dve", lambda e, x=x: e.tensor_scalar(x, x, 0.0, None, ALU.max)),
                    ("dve", lambda e, x=x: e.scalar_tensor_tensor(x, q_[:], 2.0, x, ALU.mult, ALU.add)),
                    ("dve", lambda e, x=x, h=h: e.tensor_tensor(du[:, :, h * (T // 2):(h + 1) * (T // 2)], x,
                                                                u[:, :, h * (T // 2):(h + 1) * (T // 2)], ALU.mult))]
            steps(k, "chain", ops)
    y = k.sb(f"y{b}", [P, CI, T], ctx=ctx)
    scan(k, b, A, delta, du, u, c_hm, c_lo, diag, zs, y, ctx)
    tiles = []
    for h in range(CPB):
        for m in range(C):
            prods = [(w_out[:, c, m * P:(m + 1) * P], y[:, c, h * W:(h + 1) * W]) for c in range(CI)]
            x = X[:, m, b * T + h * W:b * T + (h + 1) * W]
            tiles.append(Tile(prods, "dve", lambda e, bank, x=x: e.tensor_tensor(x, x, bank, ALU.add)))
    project(k, tiles)


def scan(k, b, A, delta, du, u, c_hm, c_lo, diag, zs, y, ctx):
    nc, ps = k.nc, k.ps
    UN = 2
    LOOPS = DS // UN
    b_bc = k.sb(f"b_bc{b}", [P, 4, W], ctx=ctx)
    dbu = k.sb(f"dbu{b}", [P, UN, CI, W], ctx=ctx)
    hs = k.sb(f"hs{b}", [P, CI, W], ctx=ctx)
    hc = k.sb(f"hc{b}", [P, UN, CI, W], ctx=ctx)
    carry = k.sb(f"carry{b}", [P, DS, CI], ctx=ctx)
    b_here = [k.sig("b_here0"), k.sig("b_here1"), k.sig("b_here2"), k.sig("b_here3")]
    decay, decay_used, dbu_ready, c_ready = k.sig("decay"), k.sig("decay_used"), k.sig("dbu_ready"), k.sig("c_ready")
    scanned, hc_ready, hc_summed, carried = k.sig("scanned"), k.sig("hc_ready"), k.sig("hc_summed"), k.sig("carried")
    y_ready, gated = k.sig("y_ready"), k.sig("gated")
    ACC, DEC, CB = 0, 4, 6

    for q in range(CPB):
        lo = q * W
        with nc.Block() as block:
            @block.sync
            def _(sp):
                for j in range(4):
                    sp.dma_start(b_bc[:, j, :], k.b_rows[b, j:j + 1, lo:lo + W].broadcast_to([P, W]))\
                        .then_inc(b_here[j].sem, 16)
                with sp.Fori(0, DS // 4 - 1) as i:
                    for j in range(4):
                        sp.wait_ge(dbu_ready.sem, i * 4 + dbu_ready.at(j + 1))
                        sp.dma_start(b_bc[:, j, :], k.b_rows[b, bass.ds(i * 4 + (4 + j), 1), lo:lo + W].broadcast_to([P, W]))\
                            .then_inc(b_here[j].sem, 16)

            @block.gpsimd
            def _(pool):
                with pool.Fori(0, DS // 4) as i:
                    for j in range(4):
                        pool.wait_ge(b_here[j].sem, i * 16 + b_here[j].at(16))
                        pool.wait_ge(scanned.sem, i * 4 + scanned.at(j + 1))
                        pool.tensor_tensor(dbu[:, j % UN, :, :], du[:, :, lo:lo + W], spread(b_bc[:, j, :], CI),
                                           ALU.mult).then_inc(dbu_ready.sem, 1)

            @block.scalar
            def _(act):
                with act.Fori(0, LOOPS) as i:
                    for j in range(UN):
                        for c in range(CI):
                            act.wait_ge(decay_used.sem, i * (UN * CI) + decay_used.at(j * CI + c + 1))
                            act.activation(ps[:, DEC + c % 2, :], delta[:, c, lo:lo + W], ACT.Exp,
                                           scale=A[:, c, bass.ds(i * UN + j, 1)]).then_inc(decay.sem, 1)

            @block.vector
            def _(dve):
                dve.sem_inc(scanned.sem, 2)
                dve.sem_inc(decay_used.sem, 2)
                if q == 0:
                    dve.memset(carry[:], 0.0).then_inc(carried.sem, 1)
                    dve.wait_ge(carried.sem, carried.at(1))
                    carried.passed(1)
                with dve.Fori(0, LOOPS) as i:
                    for j in range(UN):
                        dve.wait_ge(dbu_ready.sem, i * UN + dbu_ready.at(j + 1))
                        for c in range(CI):
                            dve.wait_ge(decay.sem, i * (UN * CI) + decay.at(j * CI + c + 1))
                            if c == 0:
                                dve.wait_ge(hc_ready.sem, i * UN + hc_ready.at(j + 1))
                            last = dve.tensor_tensor_scan(hs[:, c, :], ps[:, DEC + c % 2, :], dbu[:, j, c, :],
                                                          carry[:, bass.ds(i * UN + j, 1), c],
                                                          ALU.mult, ALU.add)
                            last.then_inc(decay_used.sem, 1)
                        dve.wait_ge(decay_used.sem, i * (UN * CI) + decay_used.at((j + 1) * CI + 2))
                        dve.tensor_scalar(carry[:, bass.ds(i * UN + j, 1), :], hs[:, :, W - 1:W].rearrange("p c o -> p o c"),
                                          1.0, None, ALU.mult)\
                            .then_inc(scanned.sem, 1)
                        dve.wait_ge(c_ready.sem, i * UN + c_ready.at(j + 1))
                        dve.wait_ge(hc_summed.sem, i * UN + hc_summed.at(j + 1))
                        dve.tensor_tensor(hc[:, j, :, :], hs[:], spread(ps[:, CB + j, :], CI), ALU.mult)\
                            .then_inc(hc_ready.sem, 1)
                for c in range(CI):
                    dve.wait_ge(y_ready.sem, y_ready.at(1))
                    dve.tensor_tensor(y[:, c, lo:lo + W], zs[:, c, lo:lo + W], ps[:, ACC + c, :], ALU.mult)\
                        .then_inc(gated.sem, 1)
                dve.wait_ge(scanned.sem, scanned.at(DS + 2))

            @block.tensor
            def _(pe):
                pe.sem_inc(hc_ready.sem, 1)
                pe.sem_inc(hc_summed.sem, 2)
                for c in range(CI):
                    pe.matmul(ps[:, ACC + c, :], diag[:, c, :], u[:, c, lo:lo + W], start=True, stop=False,
                              skip_group_check=True)
                with pe.Fori(0, LOOPS) as i:
                    for j in range(UN):
                        pe.wait_ge(hc_summed.sem, i * UN + hc_summed.at(j + 1))
                        pe.matmul(ps[:, CB + j, :], k.sel2[:, bass.ds(i * UN + j, 1)].broadcast_to([P, P]),
                                  c_hm[:, lo:lo + W], start=True, stop=False)
                        pe.matmul(ps[:, CB + j, :], k.sel2[0:DS, bass.ds(i * UN + j, 1)].broadcast_to([DS, P]),
                                  c_lo[:, lo:lo + W], start=False, stop=True).then_inc(c_ready.sem, 1)
                        pe.wait_ge(hc_ready.sem, i * UN + hc_ready.at(j + 2))
                        for c in range(CI):
                            mm = pe.matmul(ps[:, ACC + c, :], k.ident[:, :], hc[:, j, c, :], start=False, stop=False,
                                           skip_group_check=True)
                        mm.then_inc(hc_summed.sem, 1)
                pe.wait_ge(hc_summed.sem, hc_summed.at(DS + 2))
                pe.sem_inc(y_ready.sem, 1)
        for j in range(4):
            b_here[j].passed(DS // 4 * 16)
        decay.passed(DS * CI)
        decay_used.passed(DS * CI + 2)
        dbu_ready.passed(DS)
        c_ready.passed(DS)
        scanned.passed(DS + 2)
        hc_ready.passed(DS + 1)
        hc_summed.passed(DS + 2)
        y_ready.passed(1)
        gated.passed(CI)



SCORE_Q = (0, 0, 0, 1, 1, 1, 2)
SCORE_K = (0, 1, 2, 0, 1, 2, 0)
NSLOT = len(SCORE_Q)
MAX_ROW = NSLOT * DK


def split_heads(k, x, scale, parts, rows8, dram, cols):
    split = k.sig("split")
    with ExitStack() as ctx:
        rest = k.sb("rest", [P, C, cols], ctx=ctx)
        with k.nc.Block() as block:
            @block.scalar
            def _(act):
                act.activation(parts[:, 0, :, :], x, ACT.Copy, scale=scale).then_inc(split.sem, 1)
                act.wait_ge(split.sem, split.at(2))
                act.activation(parts[:, 1, :, :], rest[:], ACT.Copy).then_inc(split.sem, 1)

            @block.vector
            def _(dve):
                dve.wait_ge(split.sem, split.at(1))
                dve.scalar_tensor_tensor(rest[:], x, scale, parts[:, 0, :, :], ALU.mult, ALU.subtract)\
                   .then_inc(split.sem, 1)
                dve.wait_ge(split.sem, split.at(3))
                dve.tensor_tensor(parts[:, 2, :, :], rest[:], parts[:, 1, :, :], ALU.subtract).then_inc(split.sem, 1)

            @block.sync
            def _(sp):
                sp.wait_ge(split.sem, split.at(4))
                for c in range(C):
                    sp.dma_start(dram[:, c * P:(c + 1) * P, 0:cols].rearrange("s p t -> p s t"), parts[:, :, c, :])\
                      .then_inc(split.sem, 16)
                sp.wait_ge(split.sem, split.at(4 + 16 * C))
                for s in range(NSLOT):
                    part = (SCORE_Q if scale != 1.0 else SCORE_K)[s]
                    sp.dma_start(rows8[s * DK:(s + 1) * DK, :, :],
                                 dram[part, :, 0:cols].rearrange("(h p) t -> p h t", p=DK)).then_inc(split.sem, 16)
                sp.wait_ge(split.sem, split.at(4 + 16 * (C + NSLOT)))
    split.passed(4 + 16 * (C + NSLOT))


def attention(k, q, kk, v, nk, causal, dst, ctx):
    nc, ps = k.nc, k.ps
    KT = (nk + P - 1) // P
    q8 = k.sb("q8", [P, H, T], BF16, ctx=ctx)
    k8 = k.sb("k8", [P, H, nk], BF16, ctx=ctx)
    negmax = k.sb("negmax", [P, T // P, H], ctx=ctx)
    steps(k, "chain", [("pool", lambda e: e.memset(q8[96:P, :, :], 0.0)),
                       ("dve", lambda e: e.memset(k8[96:P, :, :], 1.0))])
    with ExitStack() as c2:
        parts = k.sb("parts", [P, 3, C, T], BF16, ctx=c2)
        split_heads(k, q, 0.25, parts, q8, k.q_parts, T)
        split_heads(k, kk, 1.0, parts[:, :, :, 0:nk], k8, k.k_parts, nk)

    scored, maxed = k.sig("scored"), k.sig("maxed")
    flat = ps[:, :, :].rearrange("p a b -> p (a b)")
    with nc.Block() as block:
        @block.tensor
        def _(pe):
            for t in range(T // P):
                n = (t + 1) * P if causal else nk
                with pe.Fori(0, H // 4) as i:
                    for j in range(4):
                        at = j * 2 * W
                        pe.wait_ge(maxed.sem, i * 4 + maxed.at(t * H + j - 3))
                        for o in range(0, n, W):
                            m = min(W, n - o)
                            mm = pe.matmul(flat[:, at + o:at + o + m], q8[:, bass.ds(i * 4 + j, 1), t * P:(t + 1) * P],
                                           k8[:, bass.ds(i * 4 + j, 1), o:o + m], start=True, stop=True)
                        if causal:
                            mm = pe.matmul(flat[:, at + n - P:at + n], k.ident16[:], k.late_key[:], start=False,
                                           stop=True, skip_group_check=True)
                        mm.then_inc(scored.sem, 1)

        @block.vector
        def _(dve):
            for t in range(T // P):
                n = (t + 1) * P if causal else nk
                with dve.Fori(0, H // 4) as i:
                    for j in range(4):
                        dve.wait_ge(scored.sem, i * 4 + scored.at(t * H + j + 1))
                        dve.tensor_reduce(negmax[:, t, bass.ds(i * 4 + j, 1)], flat[:, j * 2 * W:j * 2 * W + n], AX.X,
                                          ALU.max, negate=True).then_inc(maxed.sem, 1)
            dve.wait_ge(maxed.sem, maxed.at(T // P * H))
    scored.passed(T // P * H)
    maxed.passed(T // P * H)

    turned, split = k.sig("turned"), k.sig("split")
    with ExitStack() as c2:
        rest = k.sb("max_rest", [H, T], ctx=c2)
        mparts = k.sb("max_parts", [H, 3, T], BF16, ctx=c2)
        with nc.Block() as block:
            @block.tensor
            def _(pe):
                for t in range(T // P):
                    mm = pe.transpose(flat[0:H, t * P:(t + 1) * P], negmax[:, t, :], k.ident[:])
                mm.then_inc(turned.sem, 1)

            @block.vector
            def _(dve):
                m = flat[0:H, 0:T]
                dve.wait_ge(turned.sem, turned.at(1))
                dve.tensor_copy(mparts[:, 0, :], m).then_inc(split.sem, 1)
                dve.wait_ge(split.sem, split.at(1))
                dve.tensor_tensor(rest[:], m, mparts[:, 0, :], ALU.subtract).then_inc(split.sem, 1)
                dve.wait_ge(split.sem, split.at(2))
                dve.tensor_copy(mparts[:, 1, :], rest[:]).then_inc(split.sem, 1)
                dve.wait_ge(split.sem, split.at(3))
                dve.tensor_tensor(mparts[:, 2, :], rest[:], mparts[:, 1, :], ALU.subtract).then_inc(split.sem, 1)

            @block.sync
            def _(sp):
                sp.wait_ge(split.sem, split.at(4))
                sp.dma_start(k.m_parts.rearrange("s h t -> h s t"), mparts[:]).then_inc(split.sem, 16)
                sp.wait_ge(split.sem, split.at(20))
                sp.dma_start(q8[MAX_ROW:MAX_ROW + 3, :, :], k.m_parts).then_inc(split.sem, 16)
                sp.wait_ge(split.sem, split.at(36))
    turned.passed(1)
    split.passed(36)

    RING = 4
    prob = k.sb("prob", [P, RING, W], ctx=ctx)
    vh = k.sb("vh", [P, 2, KT, 2 * DK], ctx=ctx)
    osb = k.sb("osb", [2 * DK, 2, W], ctx=ctx)
    steps(k, "chain", [("pool", lambda e: e.memset(prob[:], 0.0)), ("dve", lambda e: e.memset(vh[:], 1.0))])
    score, weighed, used, v_ready = k.sig("score"), k.sig("weighed"), k.sig("used"), k.sig("v_ready")
    o_ready, o_taken = k.sig("o_ready"), k.sig("o_taken")
    stored = [k.sig("o_stored0"), k.sig("o_stored1")]
    heads = 0
    for qc in range(CPB):
        tiles = [(t, max(0, t * P - qc * W)) for t in range(min(KT, (qc + 1) * W // P) if causal else KT)]
        body = [(j, t, first) for j in range(2) for t, first in tiles]
        nb = len(body)
        krows = min(P, nk)
        with nc.Block() as block:
            @block.gpsimd
            def _(pool):
                with pool.Fori(0, H // 2) as i:
                    for j in range(2):
                        pool.wait_ge(o_ready.sem, i * 2 + o_ready.at(j - 1))
                        pool.tensor_copy(vh[:, j, :, 0:DK], v[:, :, bass.ds(i * 2 * DK + j * DK, DK)])\
                            .then_inc(v_ready.sem, 1)

            @block.tensor
            def _(pe):
                with pe.Fori(0, H // 2) as i:
                    def scores(n):
                        j, t, first = body[n]
                        pe.wait_ge(weighed.sem, i * nb + weighed.at(n - RING + 1))
                        diag = causal and t * P >= qc * W
                        bank = ps[0:krows, n % RING, first:W]
                        mm = pe.matmul(bank, k8[:, bass.ds(i * 2 + j, 1), t * P:t * P + krows],
                                       q8[:, bass.ds(i * 2 + j, 1), qc * W + first:(qc + 1) * W],
                                       start=True, stop=True)
                        if diag:
                            mm = pe.matmul(ps[:, n % RING, first:first + P], k.ident16[:], k.early_query[:],
                                           start=False, stop=True, skip_group_check=True)
                        mm.then_inc(score.sem, 1)

                    def sums(n):
                        j, t, first = body[n]
                        pe.wait_ge(weighed.sem, i * nb + weighed.at(n + 1))
                        if t == 0:
                            pe.wait_ge(v_ready.sem, i * 2 + v_ready.at(j + 1))
                            pe.wait_ge(o_taken.sem, i * 2 + o_taken.at(j - 1))
                        mm = pe.matmul(ps[0:2 * DK, RING + j, first:W], vh[:, j, t, :], prob[:, n % RING, first:W],
                                       start=(t == 0), stop=(t == tiles[-1][0]), skip_group_check=True)
                        mm.then_inc(used.sem, 1)
                        if t == tiles[-1][0]:
                            pe.wait_ge(used.sem, i * nb + used.at(n + 1))
                            pe.sem_inc(o_ready.sem, 1)

                    for n in range(min(3, nb)):
                        scores(n)
                    for n in range(nb):
                        sums(n)
                        if n + 3 < nb:
                            scores(n + 3)

            @block.scalar
            def _(act):
                with act.Fori(0, H // 2) as i:
                    for n, (j, t, first) in enumerate(body):
                        act.wait_ge(score.sem, i * nb + score.at(n + 1))
                        act.wait_ge(used.sem, i * nb + used.at(n - RING + 1))
                        act.activation(prob[0:krows, n % RING, first:W], ps[0:krows, n % RING, first:W], ACT.Exp)\
                           .then_inc(weighed.sem, 1)

            @block.vector
            def _(dve):
                with dve.Fori(0, H // 2) as i:
                    for j in range(2):
                        dve.wait_ge(o_ready.sem, i * 2 + o_ready.at(j + 1))
                        dve.wait_ge(stored[j].sem, i * 32 + stored[j].at(0))
                        dve.tensor_copy(osb[:, j, :], ps[0:2 * DK, RING + j, :]).then_inc(o_taken.sem, 1)

            @block.sync
            def _(sp):
                with sp.Fori(0, H // 2) as i:
                    for j in range(2):
                        sp.wait_ge(o_taken.sem, i * 2 + o_taken.at(j + 1))
                        sp.dma_start(k.o_rows[bass.ds(i * 2 * DK + j * DK, DK), qc * W:(qc + 1) * W], osb[0:DK, j, :])\
                          .then_inc(stored[j].sem, 16)
                        sp.dma_start(k.den_rows[bass.ds(i * 2 + j, 1), qc * W:(qc + 1) * W], osb[DK:DK + 1, j, :])\
                          .then_inc(stored[j].sem, 16)
                for j in range(2):
                    sp.wait_ge(stored[j].sem, stored[j].at(H // 2 * 32))
        for s in (score, weighed, used):
            s.passed(H // 2 * nb)
        for s in (v_ready, o_ready, o_taken):
            s.passed(H)
        for s in stored:
            s.passed(H // 2 * 32)

    with ExitStack() as c2:
        den = k.sb("den", [P, H * T // P], ctx=c2)
        rden = k.sb("rden", [P, C, T], ctx=c2)
        load(k, [(den[:], k.den_rows.rearrange("h (a t) -> (h a) t", t=H * T // P)),
                 (dst, k.o_rows.rearrange("(c p) t -> p c t", p=P))])
        steps(k, "chain", [("dve", lambda e: e.reciprocal(den[:], den[:]))])
        load(k, [(k.den_rows.rearrange("h (a t) -> (h a) t", t=H * T // P), den[:])])
        load(k, [(rden[DK * h:DK * h + DK, c, :], k.den_rows[8 * c + h:8 * c + h + 1, :].broadcast_to([DK, T]))
                 for c in range(C) for h in range(P // DK)])
        steps(k, "chain", [("dve", lambda e: e.tensor_tensor(dst, dst, rden[:], ALU.mult))])


def add_bank(x):
    return lambda eng, bank: eng.tensor_tensor(x, x, bank, ALU.add)


def cross(k, a):
    X = k.X
    with ExitStack() as ctx:
        XN = k.sb("XN", [P, C, N], ctx=ctx)
        norm(k, X, XN)
        w = [k.sb(n, [P, C, D], ctx=ctx) for n in ("wq", "wk", "wv", "wo")]
        cx = k.sb("cx", [P, C, B * S2], ctx=ctx)
        load(k, [(cx[:], a["ctx"])] + [(t[:], a["cross_" + n]) for t, n in zip(w, "qkvo")])
        for b in range(B):
            with ExitStack() as c2:
                q = k.sb("q", [P, C, T], ctx=c2)
                kk = k.sb("kk", [P, C, S2], ctx=c2)
                v = k.sb("v", [P, 1, D], ctx=c2)
                o = k.sb("o", [P, C, T], ctx=c2)
                steps(k, "chain", [("dve", lambda e: e.memset(v[:], 0.0))])
                tiles = []
                for m in range(C):
                    cols = slice(m * P, (m + 1) * P)
                    for h in range(CPB):
                        prods = [(w[0][:, c, cols], XN[:, c, b * T + h * W:b * T + (h + 1) * W]) for c in range(C)]
                        tiles.append(Tile(prods, "act", copy_to(q[:, m, h * W:(h + 1) * W])))
                    prods = [(w[1][:, c, cols], cx[:, c, b * S2:(b + 1) * S2]) for c in range(C)]
                    tiles.append(Tile(prods, "dve", dve_copy_to(kk[:, m, :]), cols=S2))
                prods = [(cx[:, c, b * S2:(b + 1) * S2], w[2][:, c, :]) for c in range(C)]
                tiles.append(Tile(prods, "dve", dve_copy_to(v[0:S2, 0, :]), rows=S2, cols=D))
                project(k, tiles)
                attention(k, q[:], kk[:], v, S2, False, o[:], c2)
                tiles = []
                for m in range(C):
                    for h in range(CPB):
                        prods = [(w[3][:, c, m * P:(m + 1) * P], o[:, c, h * W:(h + 1) * W]) for c in range(C)]
                        tiles.append(Tile(prods, "dve", add_bank(X[:, m, b * T + h * W:b * T + (h + 1) * W])))
                project(k, tiles)



def decoder(k, a):
    X = k.X
    with ExitStack() as ctx:
        H2 = k.sb("H2", [P, C, N], ctx=ctx)
        norm(k, X, H2)
        vec = k.sb("ffn_vec", [P, C, 4 + TAPS], ctx=ctx)
        load(k, [(vec[:], a["ffn_vec"])])
        with ExitStack() as c1:
            HN = k.sb("HN", [P, C, N], ctx=c1)
            norm(k, H2, HN, weight=vec[:, :, 0], bias=vec[:, :, 1])
            w = k.sb("w_attn", [P, C, 5 * D], ctx=c1)
            wo = k.sb("w_proj", [P, C, D], ctx=c1)
            rope = k.sb("rope", [P, 2, T], ctx=c1)
            load(k, [(w[:], a["ffn_attn"]), (wo[:], a["ffn_proj"]), (rope[:], a["rope"])])
            for b in range(B):
                with ExitStack() as c2:
                    causal_batch(k, b, HN, H2, vec, w, wo, rope, c2)
        experts(k, a, H2, vec)


def causal_batch(k, b, HN, H2, vec, w, wo, rope, ctx):
    q = k.sb("q", [P, C, T], ctx=ctx)
    kk = k.sb("kk", [P, C, T], ctx=ctx)
    v = k.sb("v", [P, T // P, D], ctx=ctx)
    with ExitStack() as c2:
        hc = k.sb("hc", [P, C, T], ctx=c2)
        turned = k.sb("turned_qk", [P, 2, C, T], ctx=c2)
        ops = []
        for c in range(C):
            x = HN[:, c, b * T:(b + 1) * T]
            ops.append(("dve", lambda e, c=c, x=x: e.tensor_scalar(hc[:, c, :], x, vec[:, c, 6:7], None, ALU.mult)))
            for d in (1, 2):
                ops.append(("dve", lambda e, c=c, x=x, d=d: e.scalar_tensor_tensor(
                    hc[:, c, d:T], x[:, 0:T - d], vec[:, c, 6 - d:7 - d], hc[:, c, d:T], ALU.mult, ALU.add)))
        steps(k, "chain", ops)
        tiles = []
        for h in range(CPB):
            cols = slice(h * W, (h + 1) * W)
            for n, (dst, table) in enumerate(((q, 0), (turned[:, 0], 1), (kk, 0), (turned[:, 1], 1))):
                for m in range(C):
                    prods = [(w[:, c, n * D + m * P:n * D + (m + 1) * P], hc[:, c, cols]) for c in range(C)]
                    tiles.append(Tile(prods, "dve", lambda e, bank, dst=dst, m=m, table=table, cols=cols:
                                      e.tensor_tensor(dst[:, m, cols], bank, rope[:, table, cols], ALU.mult)))
            for t in range(4 * h, 4 * h + 4):
                prods = [(hc[:, c, t * P:(t + 1) * P], w[:, c, 4 * D:5 * D]) for c in range(C)]
                tiles.append(Tile(prods, "act", copy_to(v[:, t, :]), cols=D))
        project(k, tiles)
        steps(k, "chain", [("dve", lambda e: e.tensor_tensor(q[:], q[:], turned[:, 0], ALU.add)),
                           ("pool", lambda e: e.tensor_tensor(kk[:], kk[:], turned[:, 1], ALU.add))])
    o = k.sb("o", [P, C, T], ctx=ctx)
    attention(k, q[:], kk[:], v, T, True, o[:], ctx)
    tiles = []
    for m in range(C):
        for h in range(CPB):
            prods = [(wo[:, c, m * P:(m + 1) * P], o[:, c, h * W:(h + 1) * W]) for c in range(C)]
            tiles.append(Tile(prods, "dve", add_bank(H2[:, m, b * T + h * W:b * T + (h + 1) * W])))
    project(k, tiles)


def experts(k, a, H2, vec):
    nc, ps, X = k.nc, k.ps, k.X
    FT = FF // P
    with ExitStack() as ctx:
        HN = k.sb("HN", [P, C, N], ctx=ctx)
        wr = k.sb("w_router", [P, C, E_], ctx=ctx)
        wv = k.sb("w_wv", [P, E_, C, 2 * FF], ctx=ctx)
        wp = k.sb("w_down", [P, E_, FT, D], ctx=ctx)
        norm(k, H2, HN, weight=vec[:, :, 2], bias=vec[:, :, 3])
        add_into(k, X, H2)
        load(k, [(wr[:], a["router"]), (wv[:], a["expert_wv"]), (wp[:], a["expert_proj"])])
        logits = k.sb("logits", [P, N // P, E_], ctx=ctx)
        tiles = []
        for t in range(N // P):
            prods = [(HN[:, c, t * P:(t + 1) * P], wr[:, c, :]) for c in range(C)]
            tiles.append(Tile(prods, "dve", dve_copy_to(logits[:, t, :]), cols=E_))
        project(k, tiles)
        best = k.sb("best", [P, N // P], ctx=ctx)
        free = k.sb("free", [P, N // P], ctx=ctx)
        pick = k.sb("pick", [P, N // P, E_], ctx=ctx)
        best_b = best[:].rearrange("p (t a) -> p t a", a=1).broadcast_to([P, N // P, E_])
        ops = [("dve", lambda e: e.tensor_reduce(best[:], logits[:], AX.X, ALU.max)),
               ("dve", lambda e: e.tensor_tensor(pick[:], logits[:], best_b, ALU.is_ge)),
               ("dve", lambda e: e.memset(free[:], 1.0))]
        for x in range(1, E_):
            ops += [("dve", lambda e, x=x: e.tensor_tensor(free[:], free[:], pick[:, :, x - 1], ALU.subtract)),
                    ("dve", lambda e, x=x: e.tensor_tensor(pick[:, :, x], pick[:, :, x], free[:], ALU.mult))]
        steps(k, "chain", ops)
        hm = k.sb("hm", [P, 2, C, W], ctx=ctx)
        gate = k.sb("gate", [P, 2, W], ctx=ctx)
        hid = k.sb("hid", [P, 2, W], ctx=ctx)
        cover, covered, cleared, pair = k.sig("cover"), k.sig("covered"), k.sig("cleared"), k.sig("pair")
        gated, hidden, summed_down, moe_out = k.sig("gated"), k.sig("hidden"), k.sig("down"), k.sig("moe_out")
        ACC, GV, MASK = 0, 2, 6
        for ch in range(NCH):
            cols = slice(ch * W, (ch + 1) * W)
            with nc.Block() as block:
                @block.tensor
                def _(pe):
                    def spread_mask(e):
                        if e >= 2:
                            pe.wait_ge(cleared.sem, cleared.at(e - 1))
                        for t in range(4):
                            mm = pe.matmul(ps[:, MASK + e % 2, t * P:(t + 1) * P],
                                           pick[:, 4 * ch + t, e:e + 1].broadcast_to([P, P]), k.ident[:],
                                           start=True, stop=True)
                        mm.then_inc(cover.sem, 1)

                    def gate_value(n):
                        e, f = divmod(n, FT)
                        if f == 0:
                            pe.wait_ge(cleared.sem, cleared.at(e + 1))
                        if n >= 2:
                            pe.wait_ge(hidden.sem, hidden.at(n - 1))
                        for g in range(2):
                            for c in range(C):
                                mm = pe.matmul(ps[:, GV + 2 * (n % 2) + g, :],
                                               wv[:, e, c, g * FF + f * P:g * FF + (f + 1) * P], hm[:, e % 2, c, :],
                                               start=(c == 0), stop=(c == C - 1))
                        mm.then_inc(pair.sem, 1)

                    def down(n):
                        e, f = divmod(n, FT)
                        pe.wait_ge(hidden.sem, hidden.at(n + 1))
                        for m in range(C):
                            mm = pe.matmul(ps[:, ACC + m, :], wp[:, e, f, m * P:(m + 1) * P], hid[:, n % 2, :],
                                           start=(n == 0), stop=(n == E_ * FT - 1), skip_group_check=True)
                        mm.then_inc(summed_down.sem, 1)

                    spread_mask(0)
                    spread_mask(1)
                    gate_value(0)
                    for n in range(E_ * FT):
                        if n + 1 < E_ * FT:
                            if (n + 1) % FT == 0 and (n + 1) // FT + 1 < E_:
                                spread_mask((n + 1) // FT + 1)
                            gate_value(n + 1)
                        down(n)

                @block.vector
                def _(dve):
                    def clear(e):
                        dve.wait_ge(cover.sem, cover.at(e + 1))
                        if e >= 2:
                            dve.wait_ge(pair.sem, pair.at((e - 1) * FT))
                        dve.tensor_tensor(hm[:, e % 2], HN[:, :, cols], spread(ps[:, MASK + e % 2, :], C), ALU.mult)\
                           .then_inc(cleared.sem, 1)

                    clear(0)
                    clear(1)
                    for n in range(E_ * FT):
                        e, f = divmod(n, FT)
                        if f == 0 and 1 <= e < E_ - 1:
                            clear(e + 1)
                        dve.wait_ge(gated.sem, gated.at(n + 1))
                        if n >= 2:
                            dve.wait_ge(summed_down.sem, summed_down.at(n - 1))
                        dve.tensor_tensor(hid[:, n % 2, :], gate[:, n % 2, :], ps[:, GV + 2 * (n % 2) + 1, :], ALU.mult)\
                           .then_inc(hidden.sem, 1)
                    dve.wait_ge(summed_down.sem, summed_down.at(E_ * FT))
                    dve.tensor_tensor(X[:, :, cols], X[:, :, cols], ps[:, ACC:ACC + 2, :], ALU.add).then_inc(moe_out.sem, 1)

                @block.scalar
                def _(act):
                    for n in range(E_ * FT):
                        act.wait_ge(pair.sem, pair.at(n + 1))
                        if n >= 2:
                            act.wait_ge(hidden.sem, hidden.at(n - 1))
                        act.activation(gate[:, n % 2, :], ps[:, GV + 2 * (n % 2), :], ACT.Silu).then_inc(gated.sem, 1)
            for s in (cover, cleared):
                s.passed(E_)
            for s in (pair, gated, hidden, summed_down):
                s.passed(E_ * FT)
            moe_out.passed(1)



def linear(k, a):
    nc, ps, X = k.nc, k.ps, k.X
    with ExitStack() as ctx:
        XN = k.sb("XN", [P, C, N], ctx=ctx)
        norm(k, X, XN)
        w = k.sb("w_qkv", [P, C, 3 * D], ctx=ctx)
        wo = k.sb("w_lproj", [P, C, D], ctx=ctx)
        bias = k.sb("lbias", [P, C], ctx=ctx)
        same = k.sb("same_head", [P, P], ctx=ctx)
        load(k, [(w[:], a["lin_qkv"]), (wo[:], a["lin_proj"]), (bias[:], a["lin_bias"]), (same[:], a["same_head"])])
        q = k.sb("lq", [P, C, N], ctx=ctx)
        o = k.sb("lo", [P, C, N], ctx=ctx)
        kt = k.sb("lk", [P, N // P, D + 1], ctx=ctx)
        vt = k.sb("lv", [P, N // P, D], ctx=ctx)
        tiles = []
        for t in range(N // P):
            prods = [(XN[:, c, t * P:(t + 1) * P], w[:, c, D:3 * D]) for c in range(C)]
            tiles.append(Tile(prods, "act", lambda e, bank, t=t: e.activation(kt[:, t, 0:D], bank[:, 0:D], ACT.Relu)))
            tiles.append(Tile([(XN[:, c, t * P:(t + 1) * P], w[:, c, 2 * D:3 * D]) for c in range(C)], "dve",
                              dve_copy_to(vt[:, t, :]), cols=D))
            tiles[-2].cols = D
            tiles[-2].products = [(l, r[:, 0:D]) for l, r in prods]
        for h in range(NCH):
            for m in range(C):
                prods = [(w[:, c, m * P:(m + 1) * P], XN[:, c, h * W:(h + 1) * W]) for c in range(C)]
                tiles.append(Tile(prods, "act", copy_to(q[:, m, h * W:(h + 1) * W], ACT.Relu)))
        project(k, tiles)
        ctxw = k.sb("ctxw", [P, B, C, P], ctx=ctx)
        ksw = k.sb("ksw", [P, B, C, P], ctx=ctx)
        ones = k.sb("lones", [P, P], ctx=ctx)
        steps(k, "chain", [("dve", lambda e: e.memset(ones[:], 1.0))])
        tiles = []
        for b in range(B):
            for c in range(C):
                tok = range(b * T // P, (b + 1) * T // P)
                kc = slice(c * P, (c + 1) * P)
                for dst, right in ((ctxw, [vt[:, t, kc] for t in tok]), (ksw, [ones[:] for t in tok])):
                    tiles.append(Tile([(kt[:, t, kc], r) for t, r in zip(tok, right)], "dve",
                                      lambda e, bank, dst=dst, b=b, c=c: e.tensor_tensor(dst[:, b, c, :], bank, same[:],
                                                                                         ALU.mult), cols=P))
        project(k, tiles)
        rz = k.sb("rz", [P, C, N], ctx=ctx)
        tiles = []
        for h in range(NCH):
            b = h // CPB
            cols = slice(h * W, (h + 1) * W)
            for c in range(C):
                tiles.append(Tile([(ctxw[:, b, c, :], q[:, c, cols])], "act", copy_to(o[:, c, cols])))
                tiles.append(Tile([(ksw[:, b, c, :], q[:, c, cols])], "dve", lambda e, bank, c=c, cols=cols:
                                  e.tensor_scalar(rz[:, c, cols], bank, EPS_F32, None, ALU.add)))
        project(k, tiles)
        steps(k, "chain", [("dve", lambda e: e.reciprocal(rz[:], rz[:])),
                           ("dve", lambda e: e.tensor_tensor(o[:], o[:], rz[:], ALU.mult))])
        tiles = []
        for h in range(NCH):
            cols = slice(h * W, (h + 1) * W)
            for m in range(C):
                prods = [(wo[:, c, m * P:(m + 1) * P], o[:, c, cols]) for c in range(C)]
                tiles.append(Tile(prods, "dve", lambda e, bank, m=m, cols=cols: e.scalar_tensor_tensor(
                    X[:, m, cols], bank, bias[:, m:m + 1], X[:, m, cols], ALU.add, ALU.add)))
        project(k, tiles)


def cross_one(k, a):
    nc, ps, X = k.nc, k.ps, k.X
    G = W // P
    with ExitStack() as ctx:
        XN = k.sb("XN", [P, C, N], ctx=ctx)
        norm(k, X, XN)
        w = k.sb("w_one", [P, C, D], ctx=ctx)
        bias = k.sb("one_bias", [P, C], ctx=ctx)
        cx = k.sb("cx", [P, C, B * S2], ctx=ctx)
        ct = k.sb("ct", [P, B, D], ctx=ctx)
        mask_in = k.sb("mask_in", [P, B, S2], I32, ctx=ctx)
        mask = k.sb("mask", [P, B, S2], ctx=ctx)
        steps(k, "chain", [("dve", lambda e: e.memset(ct[:], 0.0))])
        load(k, [(w[:], a["one_w"]), (bias[:], a["one_bias"]), (cx[:], a["ctx"]), (ct[0:S2, :, :], a["ctx_rows"])]
             + [(mask_in[:, b, :], a["mask"][b:b + 1, :].broadcast_to([P, S2])) for b in range(B)])
        yp = k.sb("yp", [P, C, B * S2], ctx=ctx)
        xp = k.sb("xp", [P, C, N], ctx=ctx)
        steps(k, "chain", [("dve", lambda e: e.tensor_copy(mask[:], mask_in[:])),
                           ("dve", lambda e: e.tensor_scalar(mask[:], mask[:], -3e38, 10.0, ALU.mult, ALU.mult))])
        tiles = []
        for m in range(C):
            relu = lambda dst, m: (lambda e, bank: e.activation(dst, bank, ACT.Relu, bias=bias[:, m:m + 1]))
            tiles.append(Tile([(w[:, c, m * P:(m + 1) * P], cx[:, c, :]) for c in range(C)], "act",
                              relu(yp[:, m, :], m), cols=B * S2))
            for h in range(NCH):
                prods = [(w[:, c, m * P:(m + 1) * P], XN[:, c, h * W:(h + 1) * W]) for c in range(C)]
                tiles.append(Tile(prods, "act", relu(xp[:, m, h * W:(h + 1) * W], m)))
        project(k, tiles)
        sc = k.sb("sc", [P, NCH, G, S2], ctx=ctx)
        top = k.sb("top", [P, NCH, G], ctx=ctx)
        pt = k.sb("pt", [P, NCH, W], ctx=ctx)
        tiles = []
        for h in range(NCH):
            b = h // CPB
            for g in range(G):
                t = h * G + g
                prods = [(xp[:, c, t * P:(t + 1) * P], yp[:, c, b * S2:(b + 1) * S2]) for c in range(C)]
                tiles.append(Tile(prods, "dve", lambda e, bank, b=b, h=h, g=g: e.tensor_tensor(
                    sc[:, h, g, :], bank, mask[:, b, :], ALU.add), cols=S2))
        project(k, tiles)
        flat = sc[:].rearrange("p h g s -> p (h g) s")
        tflat = top[:].rearrange("p h g -> p (h g)")
        tb = top[:].rearrange("p h (g a) -> p (h g) a", a=1).broadcast_to([P, NCH * G, S2])
        steps(k, "chain", [("dve", lambda e: e.tensor_reduce(tflat, flat, AX.X, ALU.max)),
                           ("dve", lambda e: e.tensor_tensor(flat, flat, tb, ALU.subtract)),
                           ("act", lambda e: e.activation(flat, flat, ACT.Exp)),
                           ("dve", lambda e: e.tensor_reduce(tflat, flat, AX.X, ALU.add)),
                           ("dve", lambda e: e.reciprocal(tflat, tflat)),
                           ("dve", lambda e: e.tensor_tensor(flat, flat, tb, ALU.mult)),
                           ("dve", lambda e: e.memset(pt[:], 0.0))])
        turned, copied = k.sig("turned"), k.sig("pt_copied")
        with nc.Block() as block:
            @block.tensor
            def _(pe):
                for h in range(NCH):
                    for g in range(G):
                        mm = pe.transpose(ps[0:S2, h, g * P:(g + 1) * P], sc[:, h, g, :], k.ident[:])
                    mm.then_inc(turned.sem, 1)

            @block.scalar
            def _(act):
                for h in range(NCH):
                    act.wait_ge(turned.sem, turned.at(h + 1))
                    act.activation(pt[0:S2, h, :], ps[0:S2, h, :], ACT.Copy).then_inc(copied.sem, 1)
        turned.passed(NCH)
        copied.passed(NCH)
        tiles = []
        for h in range(NCH):
            for m in range(C):
                tiles.append(Tile([(ct[:, h // CPB, m * P:(m + 1) * P], pt[:, h, :])], "dve",
                                  add_bank(X[:, m, h * W:(h + 1) * W])))
        project(k, tiles)


def ternary(k, w, n):
    with ExitStack() as ctx:
        s = k.sb("tern_s", [P, 1], ctx=ctx)
        r = k.sb("tern_r", [P, 1], ctx=ctx)
        x = k.sb("tern_x", [P, n], ctx=ctx)
        total = P * n
        MAGIC = 12582912.0
        steps(k, "chain", [("dve", lambda e: e.tensor_reduce(s[:], w, AX.X, ALU.add, apply_absolute_value=True))])
        project(k, [Tile([(k.inv[:], s[:])], "dve", lambda e, bank: e.tensor_scalar(
            r[:], bank, D / total, 1e-8, ALU.mult, ALU.max), cols=1)])
        steps(k, "chain", [("dve", lambda e: e.reciprocal(r[:], r[:])),
                           ("dve", lambda e: e.tensor_scalar(x[:], w, r[:, 0:1], MAGIC, ALU.mult, ALU.add)),
                           ("dve", lambda e: e.tensor_scalar(x[:], x[:], MAGIC, 1.0, ALU.subtract, ALU.min)),
                           ("dve", lambda e: e.tensor_scalar(x[:], x[:], -1.0, None, ALU.max)),
                           ("dve", lambda e: e.tensor_tensor(x[:], x[:], w, ALU.subtract)),
                           ("dve", lambda e: e.tensor_tensor(w, w, x[:], ALU.add))])


def feed_forward(k, a):
    X = k.X
    FT = FF // P
    with ExitStack() as ctx:
        XN = k.sb("XN", [P, C, N], ctx=ctx)
        norm(k, X, XN)
        w1 = k.sb("w1", [P, C * FF], ctx=ctx)
        w2 = k.sb("w2", [P, FT * D], ctx=ctx)
        b1 = k.sb("b1", [P, FT], ctx=ctx)
        b2 = k.sb("b2", [P, C], ctx=ctx)
        load(k, [(w1[:], a["ff_w1"]), (w2[:], a["ff_w2"]), (b1[:], a["ff_b1"]), (b2[:], a["ff_b2"])])
        ternary(k, w1[:], C * FF)
        ternary(k, w2[:], FT * D)
        hid = k.sb("ff_hid", [P, FT, N], ctx=ctx)
        tiles = []
        for h in range(NCH):
            cols = slice(h * W, (h + 1) * W)
            for f in range(FT):
                prods = [(w1[:, c * FF + f * P:c * FF + (f + 1) * P], XN[:, c, cols]) for c in range(C)]
                tiles.append(Tile(prods, "act", lambda e, bank, f=f, cols=cols: e.activation(
                    hid[:, f, cols], bank, ACT.Gelu, bias=b1[:, f:f + 1])))
        project(k, tiles)
        tiles = []
        for h in range(NCH):
            cols = slice(h * W, (h + 1) * W)
            for m in range(C):
                prods = [(w2[:, f * D + m * P:f * D + (m + 1) * P], hid[:, f, cols]) for f in range(FT)]
                tiles.append(Tile(prods, "dve", lambda e, bank, m=m, cols=cols: e.scalar_tensor_tensor(
                    X[:, m, cols], bank, b2[:, m:m + 1], X[:, m, cols], ALU.add, ALU.add)))
        project(k, tiles)


STAGES = [mamba, cross, decoder, linear, cross_one, feed_forward]


def build(nc, a, out, stages=None):
    ctx = ExitStack()
    with ctx:
        k = Core(nc, ctx)
        k.ps = ctx.enter_context(nc.psum_tensor("ps", [P, 8, W], F32))
        k.X = k.sb("X", [P, C, N])
        k.ident = k.sb("ident", [P, P])
        k.sel2 = k.sb("sel2", [P, DS], BF16)
        k.inv = k.sb("inv", [P, P])
        k.eps = k.sb("eps", [P, 2])
        k.b_rows = nc.dram_tensor("b_rows", (B, DS, T), F32).ap()
        k.ident16 = k.sb("ident16", [P, P], BF16)
        k.late_key = k.sb("late_key", [P, P], BF16)
        k.early_query = k.sb("early_query", [P, P], BF16)
        k.q_parts = nc.dram_tensor("q_parts", (3, D, T), BF16).ap()
        k.k_parts = nc.dram_tensor("k_parts", (3, D, T), BF16).ap()
        k.m_parts = nc.dram_tensor("m_parts", (3, H, T), BF16).ap()
        k.o_rows = nc.dram_tensor("o_rows", (D, T), F32).ap()
        k.den_rows = nc.dram_tensor("den_rows", (H, T), F32).ap()
        masks = k.sb("masks", [P, 2, P])
        load(k, [(k.X[:], a["x"]), (k.ident[:], a["ident"]), (masks[:], a["masks"])])
        steps(k, "chain", [
            ("dve", lambda e: e.memset(k.inv[:], 1.0 / D)),
            ("dve", lambda e: e.memset(k.eps[:, 0:1], EPS)),
            ("dve", lambda e: e.memset(k.eps[:, 1:2], EPS_F32)),
            ("dve", lambda e: e.tensor_copy(k.ident16[:], k.ident[:])),
            ("dve", lambda e: e.tensor_copy(k.late_key[:], masks[:, 0, :])),
            ("dve", lambda e: e.tensor_copy(k.early_query[:], masks[:, 1, :])),
            ("dve", lambda e: e.tensor_tensor(k.sel2[:], k.ident[:, 0:DS], k.ident[:, DS:P], ALU.add)),
        ])
        ring = [k.sig(n) for n in ("maxed", "weighed", "used", "o_ready", "o_taken", "o_stored0", "o_stored1")]
        with nc.Block() as block:
            @block.sync
            def _(sp):
                for s in ring:
                    sp.sem_inc(s.sem, 16)
        for s in ring:
            s.passed(16)
        for stage in (STAGES if stages is None else stages):
            stage(k, a)
        load(k, [(out, k.X[:])])


def channels_first(x):
    import numpy as np
    x = np.asarray(x)
    x = x.reshape(-1, x.shape[-1]).T
    return np.ascontiguousarray(x.reshape(-1, P, x.shape[-1]).transpose(1, 0, 2))


def rows_first(w):
    import numpy as np
    w = np.asarray(w)
    return np.ascontiguousarray(w.reshape(-1, P, w.shape[-1]).transpose(1, 0, 2))


def columns(*vs):
    import numpy as np
    return np.ascontiguousarray(np.stack([np.asarray(v).reshape(-1, P).T for v in vs], axis=-1))


def lay_out(i):
    import numpy as np
    g = {n: np.asarray(v) for n, v in i.items()}
    a = {}
    a["x"] = channels_first(g["x"])
    a["ident"] = np.eye(P, dtype=np.float32)
    wx = g["L0_attn_W_x"].T
    a["w_in"] = rows_first(g["L0_attn_W_in"].T)
    a["w_x"] = rows_first(np.concatenate([wx, wx[:, DR + DS:]], axis=1))
    a["w_dt"] = np.ascontiguousarray(g["L0_attn_W_dt"].T)
    a["w_out"] = rows_first(g["L0_attn_W_out"].T)
    cw = g["L0_attn_conv_w"]
    a["mamba_vec"] = columns(cw[:, 0, 0], cw[:, 0, 1], cw[:, 0, 2], cw[:, 0, 3], g["L0_attn_conv_b"],
                             g["L0_attn_b_dt"], g["L0_attn_Dp"])
    a["a_log"] = rows_first(g["L0_attn_A_log"])
    a["rms_w"] = columns(g["L0_attn_norm_w"])[:, :, 0]
    late = np.where(np.arange(P)[None, :] > np.arange(P)[:, None], NEG, 0.0).astype(np.float32)
    a["masks"] = np.stack([late, late.T], axis=1)
    a["ctx"] = channels_first(g["ctx_1024"])
    a["ctx_rows"] = g["ctx_1024"].transpose(1, 0, 2)
    a["mask"] = g["mask_BxS2_bf0"].astype(np.int32)
    for n in "qkvo":
        a["cross_" + n] = rows_first(g[f"L0_xattn_W_{n}"].T)
    half = DK // 2
    wq, wk, wv = np.split(g["L0_ffn_attn_w"], 3, axis=1)

    def turn(w):
        return w.reshape(D, H, 2, half)[:, :, ::-1, :].reshape(D, D)

    a["ffn_attn"] = rows_first(np.concatenate([wq, turn(wq), wk, turn(wk), wv], axis=1))
    a["ffn_proj"] = rows_first(g["L0_ffn_proj_w"])
    freq = (np.float32(1.0) / np.float32(10000.0) ** (np.arange(0, DK, 2, dtype=np.float32) / np.float32(DK)))
    angle = (np.arange(T, dtype=np.float32)[:, None] * freq.astype(np.float32)[None, :]).astype(np.float32)
    angle = np.concatenate([angle, angle], axis=1)
    sign = np.where(np.arange(DK) < half, -1.0, 1.0)
    cos = np.tile(np.cos(angle).T, (P // DK, 1))
    sin = np.tile((np.sin(angle) * sign).T, (P // DK, 1))
    a["rope"] = np.stack([cos, sin], axis=1).astype(np.float32)
    taps = g["L0_ffn_conv_w"]
    a["ffn_vec"] = columns(g["L0_ffn_ln1_w"], g["L0_ffn_ln1_b"], g["L0_ffn_ln2_w"], g["L0_ffn_ln2_b"],
                           taps[:, 0, 0], taps[:, 0, 1], taps[:, 0, 2])
    a["router"] = rows_first(g["L0_ffn_router_w"])
    a["expert_wv"] = g["L0_ffn_expert_wv"].reshape(E_, C, P, 2 * FF).transpose(2, 0, 1, 3)
    a["expert_proj"] = g["L0_ffn_expert_proj"].reshape(E_, FF // P, P, D).transpose(2, 0, 1, 3)
    a["lin_qkv"] = rows_first(g["L1_attn_w_qkv"].T)
    a["lin_proj"] = rows_first(g["L1_attn_w_proj"].T)
    a["lin_bias"] = columns(g["L1_attn_b_proj"])[:, :, 0]
    a["same_head"] = np.kron(np.eye(P // DK), np.ones((DK, DK))).astype(np.float32)
    a["one_w"] = rows_first(g["L1_xattn_W"].T)
    a["one_bias"] = columns(g["L1_xattn_b"])[:, :, 0]
    a["ff_w1"] = rows_first(g["L1_ffn_W1"].T).reshape(P, -1)
    a["ff_w2"] = rows_first(g["L1_ffn_W2"].T).reshape(P, -1)
    a["ff_b1"] = columns(g["L1_ffn_b1"])[:, :, 0]
    a["ff_b2"] = columns(g["L1_ffn_b2"])[:, :, 0]
    return {n: np.ascontiguousarray(v) for n, v in a.items()}


def kernel(**inputs):
    import numpy as np
    import concourse.bacc as bacc
    from concourse.bass_utils import run_bass_kernel_spmd as run

    nc = bacc.Bacc("TRN2", target_bir_lowering=False, num_devices=1)
    arrays = lay_out(inputs)
    a = {n: nc.dram_tensor(f"in_{n}", v.shape, mybir.dt.from_np(v.dtype), kind="ExternalInput").ap()
         for n, v in arrays.items()}
    out = nc.dram_tensor("out", (P, C, N), F32, kind="ExternalOutput").ap()
    build(nc, a, out)
    r = run(nc, [{f"in_{n}": v for n, v in arrays.items()}], core_ids=[0])
    y = np.asarray(r.results[0]["out"])
    return np.ascontiguousarray(y.transpose(1, 0, 2).reshape(D, N).T).reshape(B, T, D)
```

```python
from contextlib import ExitStack

import concourse.bass as bass
from concourse import mybir

F32 = mybir.dt.float32
BF16 = mybir.dt.bfloat16
I32 = mybir.dt.int32
ALU = mybir.AluOpType
ACT = mybir.ActivationFunctionType
AX = mybir.AxisListType

P = 128
B, T, D = 2, 1024, 256
N = B * T
C = D // P
W = 512
NCH = N // W
CPB = T // W
DI, DS, DC, DR = 512, 64, 4, 64
CI = DI // P
H, DK = 16, 16
S2 = 77
E_, FF = 4, 1024
TAPS = 3
SLOTS = 8
EPS = 1e-5
EPS_F32 = 1.1920929e-07
NEG = -1e30
TWO_ONES = 1.0019378662109375
LOG1P = (1.0, -0.49999892711639404, 0.33329710364341736, -0.24951615929603577, 0.1966327428817749,
         -0.1526966691017151, 0.10543623566627502, -0.05637361481785774, 0.019542528316378593,
         -0.0031760570127516985)


class Signal:

    def __init__(self, sem):
        self.sem, self.base = sem, 0

    def at(self, k):
        return self.base + k

    def passed(self, k):
        self.base += k


class Core:

    def __init__(self, nc, ctx):
        self.nc, self.ctx, self.signals, self.names = nc, ctx, {}, 0

    def sb(self, name, shape, dt=F32, ctx=None):
        self.names += 1
        return (ctx or self.ctx).enter_context(self.nc.sbuf_tensor(f"{name}_{self.names}", shape, dt))

    def sig(self, name):
        if name not in self.signals:
            self.signals[name] = Signal(self.ctx.enter_context(self.nc.semaphore(name)))
        return self.signals[name]


def spread(ap, k):
    p, n = ap.shape
    return ap.rearrange("p (a n) -> p a n", a=1).broadcast_to([p, k, n])


def load(k, pairs):
    moved = k.sig("moved")
    with k.nc.Block() as block:
        @block.sync
        def _(sp):
            for dst, src in pairs:
                sp.dma_start(dst, src).then_inc(moved.sem, 16)
            sp.wait_ge(moved.sem, moved.at(16 * len(pairs)))
    moved.passed(16 * len(pairs))


def norm(k, src, dst, centre=True, eps=EPS, weight=None, bias=None, loads=(), later=(), later_in=None, fills=()):
    nc, ps = k.nc, k.ps
    mean_ready, centred, squared = k.sig("mean_ready"), k.sig("centred"), k.sig("squared")
    var_ready, root_ready, root_squared = k.sig("var_ready"), k.sig("root_ready"), k.sig("root_squared")
    newton, corrected, rstd_ready = k.sig("newton"), k.sig("corrected"), k.sig("rstd_ready")
    scaled, scaled_dve, normed, filled = k.sig("scaled"), k.sig("scaled_dve"), k.sig("normed"), k.sig("filled")
    affine = weight is not None
    with ExitStack() as ctx:
        sq = k.sb("norm_sq", [P, NCH, C, W], ctx=ctx)
        r0 = k.sb("norm_r0", [P, NCH, W], ctx=ctx)
        r0sq = k.sb("norm_r0sq", [P, NCH, W], ctx=ctx)
        rstd = k.sb("norm_rstd", [P, NCH, W], ctx=ctx)
        block = ctx.enter_context(nc.Block())
        body = dst if centre else src
        VAR = NCH
        BY_POOL = NCH // 2

        def chunk(t, c):
            return t[:, :, c * W:(c + 1) * W]

        if loads:
            moved = k.sig("moved")

            @block.sync
            def _(sp):
                for to, source in loads:
                    sp.dma_start(to, source).then_inc(moved.sem, 16)
                for to, source in later:
                    sp.dma_start(to, source).then_inc(later_in.sem, 16)
                sp.wait_ge(moved.sem, moved.at(16 * len(loads)))

        @block.tensor
        def _(pe):
            if centre:
                for c in range(NCH):
                    for b in range(C):
                        mm = pe.matmul(ps[:, c, :], k.inv[:, :], src[:, b, c * W:(c + 1) * W],
                                       start=(b == 0), stop=(b == C - 1))
                    mm.then_inc(mean_ready.sem, 1)
            for c in range(NCH):
                pe.wait_ge(squared.sem, squared.at(c + 1))
                for b in range(C):
                    mm = pe.matmul(ps[:, VAR + c, :], k.inv[:, :], sq[:, c, b, :], start=(b == 0), stop=(b == C - 1))
                mm.then_inc(var_ready.sem, 1)

        @block.vector
        def _(dve):
            if centre:
                for c in range(NCH):
                    dve.wait_ge(mean_ready.sem, mean_ready.at(c + 1))
                    dve.tensor_tensor(chunk(dst, c), chunk(src, c), spread(ps[:, c, :], C),
                                      ALU.subtract).then_inc(centred.sem, 1)
            for c in range(NCH):
                dve.wait_ge(var_ready.sem, var_ready.at(c + 1))
                dve.wait_ge(root_squared.sem, root_squared.at(c + 1))
                dve.scalar_tensor_tensor(rstd[:, c, :], ps[:, VAR + c, :], float(eps), r0sq[:, c, :],
                                         ALU.add, ALU.mult).then_inc(newton.sem, 1)
                dve.wait_ge(newton.sem, newton.at(c + 1))
                dve.tensor_scalar(rstd[:, c, :], rstd[:, c, :], -0.5, 1.5, ALU.mult, ALU.add).then_inc(corrected.sem, 1)
                dve.wait_ge(corrected.sem, corrected.at(c + 1))
                dve.tensor_tensor(rstd[:, c, :], rstd[:, c, :], r0[:, c, :], ALU.mult).then_inc(rstd_ready.sem, 1)
                if c >= BY_POOL:
                    dve.wait_ge(rstd_ready.sem, rstd_ready.at(c + 1))
                    dve.tensor_tensor(chunk(dst, c), chunk(body, c), spread(rstd[:, c, :], C),
                                      ALU.mult).then_inc(scaled_dve.sem, 1)

        @block.scalar
        def _(act):
            def affine_chunk(c):
                if c < BY_POOL:
                    act.wait_ge(scaled.sem, scaled.at(c + 1))
                else:
                    act.wait_ge(scaled_dve.sem, scaled_dve.at(c - BY_POOL + 1))
                for b in range(C):
                    x = dst[:, b, c * W:(c + 1) * W]
                    act.activation(x, x, ACT.Identity, scale=weight[:, b:b + 1],
                                   bias=bias[:, b:b + 1] if bias is not None else 0.0).then_inc(normed.sem, 1)

            for c in range(NCH):
                if centre:
                    act.wait_ge(centred.sem, centred.at(c + 1))
                act.activation(sq[:, c, :, :], chunk(body, c), ACT.Square).then_inc(squared.sem, 1)
            for c in range(NCH):
                act.wait_ge(var_ready.sem, var_ready.at(c + 1))
                act.activation(r0[:, c, :], ps[:, VAR + c, :], ACT.Abs_reciprocal_sqrt,
                               bias=k.eps[:, 0:1] if eps == EPS else k.eps[:, 1:2]).then_inc(root_ready.sem, 1)
                act.wait_ge(root_ready.sem, root_ready.at(c + 1))
                act.activation(r0sq[:, c, :], r0[:, c, :], ACT.Square).then_inc(root_squared.sem, 1)
            if affine:
                for c in range(NCH):
                    affine_chunk(c)

        @block.gpsimd
        def _(pool):
            for n, (to, value) in enumerate(fills):
                pool.memset(to, value).then_inc(filled.sem, 1)
                pool.wait_ge(filled.sem, filled.at(n + 1))
            for c in range(BY_POOL):
                pool.wait_ge(rstd_ready.sem, rstd_ready.at(c + 1))
                if not centre:
                    pool.wait_ge(squared.sem, squared.at(c + 1))
                pool.tensor_tensor(chunk(dst, c), chunk(body, c), spread(rstd[:, c, :], C),
                                   ALU.mult).then_inc(scaled.sem, 1)
            pool.wait_ge(scaled.sem, scaled.at(BY_POOL))

        ctx.pop_all().close()
    if centre:
        mean_ready.passed(NCH)
        centred.passed(NCH)
    for s in (squared, var_ready, root_ready, root_squared, newton, corrected, rstd_ready):
        s.passed(NCH)
    scaled.passed(BY_POOL)
    scaled_dve.passed(NCH - BY_POOL)
    if affine:
        normed.passed(NCH * C)
    if loads:
        moved.passed(16 * len(loads))
    filled.passed(len(fills))


class Tile:

    def __init__(self, products, engine, take, rows=P, cols=W):
        self.products, self.engine, self.take, self.rows, self.cols = products, engine, take, rows, cols


class Pending:

    def __init__(self, fetch, normalise, tiles, attended):
        self.fetch, self.normalise, self.tiles, self.attended = fetch, normalise, tiles, attended


def project(k, tiles, banks=8, pending=None):
    nc, ps = k.nc, k.ps
    own = len(tiles)
    if pending:
        tiles = tiles + pending.tiles
    summed = k.sig("summed")
    taken = {"act": k.sig("taken_act"), "dve": k.sig("taken_dve")}
    done = {"act": 0, "dve": 0}
    count = []
    for t in tiles:
        done[t.engine] += 1
        count.append(done[t.engine])
    with nc.Block() as block:
        @block.tensor
        def _(pe):
            for n, t in enumerate(tiles):
                if n >= banks:
                    old = tiles[n - banks]
                    pe.wait_ge(taken[old.engine].sem, taken[old.engine].at(count[n - banks]))
                if n == own:
                    pe.wait_ge(pending.attended.sem, pending.attended.at(1))
                for i, (lhs, rhs) in enumerate(t.products):
                    mm = pe.matmul(ps[0:t.rows, n % banks, 0:t.cols], lhs, rhs, start=(i == 0),
                                   stop=(i == len(t.products) - 1))
                mm.then_inc(summed.sem, 1)

        def take_all(eng, name):
            for n, t in enumerate(tiles):
                if pending and name == "dve" and n == min(own, banks):
                    pending.normalise(eng)
                if t.engine == name:
                    eng.wait_ge(summed.sem, summed.at(n + 1))
                    t.take(eng, ps[0:t.rows, n % banks, 0:t.cols]).then_inc(taken[name].sem, 1)

        @block.scalar
        def _(act):
            take_all(act, "act")

        @block.vector
        def _(dve):
            take_all(dve, "dve")

        if pending:
            @block.sync
            def _(sp):
                pending.fetch(sp)
    summed.passed(len(tiles))
    for name in taken:
        taken[name].passed(done[name])
    if pending:
        k.sig("fetched").passed(16 * 2 * C)
        k.sig("attended").passed(1)


def copy_to(dst, func=ACT.Copy, scale=1.0):
    return lambda eng, bank: eng.activation(dst, bank, func, scale=scale)


def dve_copy_to(dst):
    return lambda eng, bank: eng.tensor_copy(dst, bank)


def steps(k, name, ops):
    chain = k.sig(name)
    with k.nc.Block() as block:
        def run(eng, mine):
            for n, (who, call) in enumerate(ops):
                if who == mine:
                    if n:
                        eng.wait_ge(chain.sem, chain.at(n))
                    call(eng).then_inc(chain.sem, 1)
            eng.wait_ge(chain.sem, chain.at(len(ops)))

        @block.vector
        def _(dve):
            run(dve, "dve")

        @block.scalar
        def _(act):
            run(act, "act")

        @block.gpsimd
        def _(pool):
            run(pool, "pool")
    chain.passed(len(ops))


def add_into(k, x, y):
    added = k.sig("added")
    with k.nc.Block() as block:
        @block.vector
        def _(dve):
            dve.tensor_tensor(x[:, :, 0:N // 2], x[:, :, 0:N // 2], y[:, :, 0:N // 2], ALU.add)\
               .then_inc(added.sem, 1)
            dve.tensor_tensor(x[:, 0, N // 2:N], x[:, 0, N // 2:N], y[:, 0, N // 2:N], ALU.add)\
               .then_inc(added.sem, 1)
            dve.wait_ge(added.sem, added.at(3))

        @block.gpsimd
        def _(pool):
            pool.tensor_tensor(x[:, 1, N // 2:N], x[:, 1, N // 2:N], y[:, 1, N // 2:N], ALU.add)\
                .then_inc(added.sem, 1)
    added.passed(3)



def mamba(k, a):
    X = k.X
    with ExitStack() as ctx:
        XN = k.sb("XN", [P, C, N], ctx=ctx)
        w_in = k.sb("w_in", [P, C, 2 * DI], ctx=ctx)
        w_x = k.sb("w_x", [P, CI, 2 * P], ctx=ctx)
        w_dt = k.sb("w_dt", [P, DI], ctx=ctx)
        w_out = k.sb("w_out", [P, CI, D], ctx=ctx)
        vec = k.sb("mamba_vec", [P, CI, DC + 3], ctx=ctx)
        A = k.sb("A", [P, CI, DS], ctx=ctx)
        rms_w = k.sb("rms_w", [P, C], ctx=ctx)
        norm(k, X, XN, loads=[(w_in[:], a["w_in"]), (w_x[:], a["w_x"]), (w_dt[:], a["w_dt"]), (w_out[:], a["w_out"]),
                              (vec[:], a["mamba_vec"]), (A[:], a["a_log"]), (rms_w[:], a["rms_w"])])
        add_into(k, X, XN)
        norm(k, XN, XN, centre=False, eps=EPS_F32, weight=rms_w)
        diag = k.sb("diag_skip", [P, CI, P], ctx=ctx)
        for b in range(B):
            with ExitStack() as bctx:
                mamba_batch(k, b, XN, w_in, w_x, w_dt, w_out, vec, A, diag, bctx)


def mamba_batch(k, b, XN, w_in, w_x, w_dt, w_out, vec, A, diag, ctx):
    X = k.X
    zs = k.sb("zs", [P, CI, T], ctx=ctx)
    u = k.sb("u", [P, CI, T], ctx=ctx)
    delta = k.sb("delta", [P, CI, T], ctx=ctx)
    du = k.sb("du", [P, CI, T], ctx=ctx)
    c_hm = k.sb("c_hm", [P, T], BF16, ctx=ctx)
    c_lo = k.sb("c_lo", [DS, T], BF16, ctx=ctx)
    with ExitStack() as c2:
        scan_inputs(k, b, XN, w_in, w_x, w_dt, vec, A, diag, zs, u, delta, du, c_hm, c_lo, c2)
    scan(k, b, A, delta, du, u, c_hm, c_lo, diag, zs, ctx)
    tiles = []
    for h in range(CPB):
        for m in range(C):
            prods = [(w_out[:, c, m * P:(m + 1) * P], du[:, c, h * W:(h + 1) * W]) for c in range(CI)]
            x = X[:, m, b * T + h * W:b * T + (h + 1) * W]
            tiles.append(Tile(prods, "dve", add_bank(x)))
    project(k, tiles)


def scan_inputs(k, b, XN, w_in, w_x, w_dt, vec, A, diag, zs, u, delta, du, c_hm, c_lo, ctx):
    nc, ps = k.nc, k.ps
    xm = k.sb("xm", [P, CI, DC - 1 + T], ctx=ctx)
    low = k.sb("low", [P, T], ctx=ctx)
    rest = k.sb("c_rest", [P, W], ctx=ctx)
    mid = k.sb("c_mid", [P, W], BF16, ctx=ctx)
    e_ = k.sb("sp_e", [P, CPB, CI, W], ctx=ctx)
    poly = k.sb("sp_poly", [P, CPB, CI, W], ctx=ctx)
    summed, taken = k.sig("summed"), k.sig("taken_act")
    tapped, convolved, u_ready = k.sig("tapped"), k.sig("convolved"), k.sig("u_ready")
    c_split, c_taken, b_stored = k.sig("c_split"), k.sig("c_taken"), k.sig("b_stored")
    magnitude, e_ready = k.sig("magnitude"), k.sig("e_ready")
    soft = {"dve": k.sig("soft_dve"), "pool": k.sig("soft_pool")}
    SPLIT = (CI - 1, CI)
    SOFT_DVE, SOFT_POOL = len(LOG1P) + 2, 2 * len(LOG1P) + 1
    a_ready, prepared = k.sig("a_ready"), k.sig("prepared")
    order = [(kind, h, m) for kind, h, tiles in (("xm", 0, CI), ("xm", 1, CI), ("z", 0, CI), ("low", 0, 1), ("C", 0, 1),
                                                 ("delta", 0, CI), ("low", 1, 1), ("C", 1, 1), ("delta", 1, CI),
                                                 ("z", 1, CI)) for m in range(tiles)]
    index = {t: n for n, t in enumerate(order)}
    takes = [t for t in order if t[0] != "C"]
    take_no = {t: n + 1 for n, t in enumerate(takes)}

    def bank(tile):
        return ps[:, index[tile] % 8, :]

    def softplus_dve(dve, h):
        cols, part = slice(h * W, (h + 1) * W), slice(0, SPLIT[h])
        x, e, p = delta[:, part, cols], e_[:, h, part, :], poly[:, h, part, :]
        done = soft["dve"]
        n = h * SOFT_DVE
        dve.wait_ge(e_ready.sem, e_ready.at(h + 1))
        dve.tensor_scalar(p, e, LOG1P[-1], None, ALU.mult).then_inc(done.sem, 1)
        for c in LOG1P[-2::-1]:
            n += 1
            dve.wait_ge(done.sem, done.at(n))
            dve.scalar_tensor_tensor(p, p, c, e, ALU.add, ALU.mult).then_inc(done.sem, 1)
        dve.wait_ge(done.sem, done.at(n + 1))
        dve.scalar_tensor_tensor(x, x, 0.0, p, ALU.max, ALU.add).then_inc(done.sem, 1)
        dve.wait_ge(done.sem, done.at(n + 2))
        dve.tensor_tensor(du[:, part, cols], x, u[:, part, cols], ALU.mult).then_inc(done.sem, 1)

    def softplus_pool(pool, h):
        cols, part = slice(h * W, (h + 1) * W), slice(SPLIT[h], CI)
        x, e, p = delta[:, part, cols], e_[:, h, part, :], poly[:, h, part, :]
        done = soft["pool"]
        n = h * SOFT_POOL
        pool.wait_ge(e_ready.sem, e_ready.at(h + 1))
        pool.tensor_scalar(x, x, 0.0, None, ALU.max).then_inc(done.sem, 1)
        pool.tensor_scalar(p, e, LOG1P[-1], LOG1P[-2], ALU.mult, ALU.add).then_inc(done.sem, 1)
        for c in LOG1P[-3::-1]:
            n += 2
            pool.wait_ge(done.sem, done.at(n))
            pool.tensor_tensor(p, p, e, ALU.mult).then_inc(done.sem, 1)
            pool.wait_ge(done.sem, done.at(n + 1))
            pool.tensor_scalar(p, p, c, None, ALU.add).then_inc(done.sem, 1)
        pool.wait_ge(done.sem, done.at(n + 2))
        pool.tensor_tensor(p, p, e, ALU.mult).then_inc(done.sem, 1)
        pool.wait_ge(done.sem, done.at(n + 3))
        pool.tensor_tensor(x, x, p, ALU.add).then_inc(done.sem, 1)
        pool.wait_ge(done.sem, done.at(n + 4))
        pool.tensor_tensor(du[:, part, cols], x, u[:, part, cols], ALU.mult).then_inc(done.sem, 1)

    with nc.Block() as block:
        @block.tensor
        def _(pe):
            for n, (kind, h, m) in enumerate(order):
                if n >= 8:
                    old = order[n - 8]
                    if old[0] == "C":
                        pe.wait_ge(c_taken.sem, c_taken.at(old[1] + 1))
                    else:
                        pe.wait_ge(taken.sem, taken.at(take_no[old]))
                cols = slice(h * W, (h + 1) * W)
                out = ps[:, n % 8, :]
                if kind in ("xm", "z"):
                    o = (m + (CI if kind == "z" else 0)) * P
                    for c in range(C):
                        mm = pe.matmul(out, w_in[:, c, o:o + P], XN[:, c, b * T + h * W:b * T + (h + 1) * W],
                                       start=(c == 0), stop=(c == C - 1))
                elif kind == "delta":
                    if m == 0:
                        pe.wait_ge(taken.sem, taken.at(take_no["low", h, 0]))
                    mm = pe.matmul(out, w_dt[:, m * P:(m + 1) * P], low[:, cols], start=True, stop=True)
                else:
                    o = P if kind == "C" else 0
                    for c in range(CI):
                        if kind == "low":
                            pe.wait_ge(u_ready.sem, u_ready.at(h * CI + c + 1))
                        mm = pe.matmul(out, w_x[:, c, o:o + P], u[:, c, cols], start=(c == 0), stop=(c == CI - 1))
                mm.then_inc(summed.sem, 1)

        @block.scalar
        def _(act):
            def take(kind, h, m, dst, func, **kw):
                tile = (kind, h, m)
                act.wait_ge(summed.sem, summed.at(index[tile] + 1))
                act.activation(dst, bank(tile), func, **kw).then_inc(taken.sem, 1)

            def take_xm(h):
                for m in range(CI):
                    take("xm", h, m, xm[:, m, DC - 1 + h * W:DC - 1 + (h + 1) * W], ACT.Copy)

            def take_z(h):
                for m in range(CI):
                    take("z", h, m, zs[:, m, h * W:(h + 1) * W], ACT.Silu)

            def take_low(h):
                take("low", h, 0, low[:, h * W:(h + 1) * W], ACT.Copy)

            def take_delta(h):
                for m in range(CI):
                    take("delta", h, m, delta[:, m, h * W:(h + 1) * W], ACT.Identity, bias=vec[:, m, DC + 1:DC + 2])

            def silu_u(h):
                for m in range(CI):
                    act.wait_ge(convolved.sem, convolved.at(h * CI + m + 1))
                    x = u[:, m, h * W:(h + 1) * W]
                    act.activation(x, x, ACT.Silu, bias=vec[:, m, DC:DC + 1]).then_inc(u_ready.sem, 1)

            def exponential(h):
                act.wait_ge(taken.sem, taken.at(take_no["delta", h, CI - 1]))
                act.activation(e_[:, h], delta[:, :, h * W:(h + 1) * W], ACT.Abs).then_inc(magnitude.sem, 1)
                act.wait_ge(magnitude.sem, magnitude.at(h + 1))
                act.activation(e_[:, h], e_[:, h], ACT.Exp, scale=-1.0).then_inc(e_ready.sem, 1)

            if b == 0:
                act.activation(A[:], A[:], ACT.Exp).then_inc(a_ready.sem, 1)
            take_xm(0)
            take_xm(1)
            silu_u(0)
            take_z(0)
            take_low(0)
            silu_u(1)
            take_delta(0)
            exponential(0)
            take_low(1)
            take_delta(1)
            exponential(1)
            take_z(1)

        @block.vector
        def _(dve):
            def convolve(h):
                for m in range(CI):
                    x = u[:, m, h * W:(h + 1) * W]
                    dve.wait_ge(taken.sem, taken.at(take_no["xm", h, m]))
                    dve.tensor_scalar(x, xm[:, m, h * W:h * W + W], vec[:, m, 0:1], None, ALU.mult)\
                       .then_inc(tapped.sem, 1)
                    for j in range(1, DC):
                        dve.wait_ge(tapped.sem, tapped.at((h * CI + m) * (DC - 1) + j + 1))
                        dve.scalar_tensor_tensor(x, xm[:, m, h * W + j:h * W + j + W], vec[:, m, j:j + 1], x,
                                                 ALU.mult, ALU.add)\
                           .then_inc((tapped if j + 1 < DC else convolved).sem, 1)

            def split_c(h):
                cols = slice(h * W, (h + 1) * W)
                c_bank = bank(("C", h, 0))
                dve.wait_ge(summed.sem, summed.at(index["C", h, 0] + 1))
                dve.tensor_copy(c_hm[:, cols], c_bank).then_inc(c_split.sem, 1)
                dve.wait_ge(c_split.sem, c_split.at(h * 5 + 1))
                dve.tensor_tensor(rest[:], c_bank, c_hm[:, cols], ALU.subtract).then_inc(c_taken.sem, 1)
                dve.wait_ge(c_taken.sem, c_taken.at(h + 1))
                dve.tensor_copy(mid[:], rest[:]).then_inc(c_split.sem, 1)
                dve.wait_ge(c_split.sem, c_split.at(h * 5 + 2))
                dve.tensor_copy(c_hm[DS:P, cols], mid[DS:P, :]).then_inc(c_split.sem, 1)
                dve.tensor_tensor(rest[0:DS, :], rest[0:DS, :], mid[0:DS, :], ALU.subtract).then_inc(c_split.sem, 1)
                dve.wait_ge(c_split.sem, c_split.at(h * 5 + 4))
                dve.tensor_copy(c_lo[:, cols], rest[0:DS, :]).then_inc(c_split.sem, 1)

            dve.memset(xm[:, :, 0:DC - 1], 0.0).then_inc(tapped.sem, 1)
            dve.wait_ge(tapped.sem, tapped.at(1))
            convolve(0)
            convolve(1)
            for h in range(CPB):
                split_c(h)
                softplus_dve(dve, h)

        @block.gpsimd
        def _(pool):
            if b == 0:
                for c in range(CI):
                    pool.tensor_scalar(diag[:, c, :], k.ident[:, :], vec[:, c, DC + 2:DC + 3], None, ALU.mult)\
                        .then_inc(prepared.sem, 1)
                pool.wait_ge(a_ready.sem, a_ready.at(1))
                pool.tensor_scalar(A[:], A[:], -1.0, None, ALU.mult).then_inc(prepared.sem, 1)
            softplus_pool(pool, 0)
            pool.wait_ge(soft["pool"].sem, soft["pool"].at(SOFT_POOL))
            if b == 0:
                pool.wait_ge(prepared.sem, prepared.at(CI + 1))

        @block.sync
        def _(sp):
            for h in range(CPB):
                sp.wait_ge(taken.sem, taken.at(take_no["low", h, 0]))
                sp.dma_start(k.b_rows[b][:, h * W:(h + 1) * W], low[DR:P, h * W:(h + 1) * W]).then_inc(b_stored.sem, 16)
            sp.wait_ge(b_stored.sem, b_stored.at(16 * CPB))
    summed.passed(len(order))
    taken.passed(len(takes))
    tapped.passed(CPB * CI * (DC - 1) + 1)
    for s in (convolved, u_ready):
        s.passed(CPB * CI)
    c_split.passed(CPB * 5)
    soft["dve"].passed(CPB * SOFT_DVE)
    soft["pool"].passed(SOFT_POOL)
    for s in (c_taken, magnitude, e_ready):
        s.passed(CPB)
    b_stored.passed(16 * CPB)
    if b == 0:
        a_ready.passed(1)
        prepared.passed(CI + 1)


def scan(k, b, A, delta, du, u, c_hm, c_lo, diag, zs, ctx):
    nc, ps = k.nc, k.ps
    UN = 4
    LOOPS = DS // UN
    HC = CI // 2
    b_bc = k.sb(f"b_bc{b}", [P, UN, W], ctx=ctx)
    dbu = k.sb(f"dbu{b}", [P, UN, CI, W], ctx=ctx)
    hs = k.sb(f"hs{b}", [P, 2, CI, W], ctx=ctx)
    hc = k.sb(f"hc{b}", [P, 2, CI, W], ctx=ctx)
    carry = k.sb(f"carry{b}", [P, DS, CI], ctx=ctx)
    b_here = [k.sig(f"b_here{j}") for j in range(UN)]
    decay, scanned, dbu_ready, c_ready = k.sig("decay"), k.sig("scanned"), k.sig("dbu_ready"), k.sig("c_ready")
    hc_ready, hc_summed, carried = k.sig("hc_ready"), k.sig("hc_summed"), k.sig("carried")
    y_ready, gated = k.sig("y_ready"), k.sig("gated")
    ACC, DEC, CB = 0, 4, 7

    def bank_of(j, c):
        n = (j * CI + c) % (2 * CI)
        return DEC + n % 3, (2, 2, 5, 3, 3, 3, 3, 3)[n]

    for q in range(CPB):
        lo = q * W
        with nc.Block() as block:
            @block.sync
            def _(sp):
                for j in range(UN):
                    sp.dma_start(b_bc[:, j, :], k.b_rows[b, j:j + 1, lo:lo + W].broadcast_to([P, W]))\
                        .then_inc(b_here[j].sem, 16)
                with sp.Fori(0, LOOPS - 1) as i:
                    for j in range(UN):
                        sp.wait_ge(dbu_ready.sem, i * UN + dbu_ready.at(j + 1))
                        sp.dma_start(b_bc[:, j, :],
                                     k.b_rows[b, bass.ds(i * UN + (UN + j), 1), lo:lo + W].broadcast_to([P, W]))\
                            .then_inc(b_here[j].sem, 16)

            @block.gpsimd
            def _(pool):
                with pool.Fori(0, LOOPS) as i:
                    for j in range(UN):
                        pool.wait_ge(b_here[j].sem, i * 16 + b_here[j].at(16))
                        pool.wait_ge(scanned.sem, i * (UN * CI) + scanned.at((j + 1) * CI))
                        pool.tensor_tensor(dbu[:, j, :, :], du[:, :, lo:lo + W], spread(b_bc[:, j, :], CI),
                                           ALU.mult).then_inc(dbu_ready.sem, 1)

            @block.scalar
            def _(act):
                with act.Fori(0, LOOPS) as i:
                    for j in range(UN):
                        for c in range(CI):
                            bank, ago = bank_of(j, c)
                            act.wait_ge(scanned.sem, i * (UN * CI) + scanned.at((j + UN) * CI + c + 1 - ago))
                            act.activation(ps[:, bank, :], delta[:, c, lo:lo + W], ACT.Exp,
                                           scale=A[:, c, bass.ds(i * UN + j, 1)]).then_inc(decay.sem, 1)

            @block.vector
            def _(dve):
                dve.sem_inc(scanned.sem, UN * CI)

                def scans(i, j):
                    dve.wait_ge(dbu_ready.sem, i * UN + dbu_ready.at(j + 1))
                    for c in range(CI):
                        dve.wait_ge(decay.sem, i * (UN * CI) + decay.at(j * CI + c + 1))
                        if c % HC == 0:
                            dve.wait_ge(hc_ready.sem, i * (2 * UN) + hc_ready.at(2 * j + c // HC + 1))
                        dve.tensor_tensor_scan(hs[:, j % 2, c, :], ps[:, bank_of(j, c)[0], :], dbu[:, j % UN, c, :],
                                               carry[:, bass.ds(i * UN + j, 1), c] if q else 0.0, ALU.mult, ALU.add)\
                           .then_inc(scanned.sem, 1)

                def times_c(i, j):
                    dve.wait_ge(scanned.sem, i * (UN * CI) + scanned.at((j + 1 + UN) * CI))
                    if q + 1 < CPB:
                        dve.tensor_scalar(carry[:, bass.ds(i * UN + j, 1), :],
                                          hs[:, j % 2, :, W - 1:W].rearrange("p c o -> p o c"),
                                          1.0, None, ALU.mult).then_inc(carried.sem, 1)
                    dve.wait_ge(c_ready.sem, i * UN + c_ready.at(j + 1))
                    for g in range(2):
                        half = slice(g * HC, (g + 1) * HC)
                        dve.wait_ge(hc_summed.sem, i * (2 * UN) + hc_summed.at(2 * j + g + 1))
                        dve.tensor_tensor(hc[:, j % 2, half, :], hs[:, j % 2, half, :], spread(ps[:, CB, :], HC),
                                          ALU.mult).then_inc(hc_ready.sem, 1)

                scans(0, 0)
                with dve.Fori(0, LOOPS - 1) as i:
                    for j in range(UN):
                        scans(i, j + 1)
                        times_c(i, j)
                for j in range(DS - UN, DS - 1):
                    scans(0, j + 1)
                    times_c(0, j)
                times_c(0, DS - 1)
                for c in range(CI):
                    dve.wait_ge(y_ready.sem, y_ready.at(1))
                    dve.tensor_tensor(du[:, c, lo:lo + W], zs[:, c, lo:lo + W], ps[:, ACC + c, :], ALU.mult)\
                        .then_inc(gated.sem, 1)
                if q + 1 < CPB:
                    dve.wait_ge(carried.sem, carried.at(DS))

            @block.tensor
            def _(pe):
                pe.sem_inc(hc_ready.sem, 4)
                pe.sem_inc(hc_summed.sem, 4)
                for c in range(CI):
                    pe.matmul(ps[:, ACC + c, :], diag[:, c, :], u[:, c, lo:lo + W], start=True, stop=False,
                              skip_group_check=True)

                def spread_c(i, j):
                    pe.wait_ge(hc_ready.sem, i * (2 * UN) + hc_ready.at(2 * j + 4))
                    pe.matmul(ps[:, CB, :], k.sel2[:, bass.ds(i * UN + j, 1)].broadcast_to([P, P]),
                              c_hm[:, lo:lo + W], start=True, stop=False)
                    pe.matmul(ps[:, CB, :], k.sel2[0:DS, bass.ds(i * UN + j, 1)].broadcast_to([DS, P]),
                              c_lo[:, lo:lo + W], start=False, stop=True).then_inc(c_ready.sem, 1)

                def sum_states(i, j, g):
                    pe.wait_ge(hc_ready.sem, i * (2 * UN) + hc_ready.at(2 * j + g + 5))
                    for c in range(g * HC, (g + 1) * HC):
                        mm = pe.matmul(ps[:, ACC + c, :], k.ident[:, :], hc[:, j % 2, c, :], start=False, stop=False,
                                       skip_group_check=True)
                    mm.then_inc(hc_summed.sem, 1)

                spread_c(0, 0)
                with pe.Fori(0, LOOPS - 1) as i:
                    for j in range(UN):
                        sum_states(i, j, 0)
                        spread_c(i, j + 1)
                        sum_states(i, j, 1)
                for j in range(DS - UN, DS):
                    sum_states(0, j, 0)
                    if j + 1 < DS:
                        spread_c(0, j + 1)
                    sum_states(0, j, 1)
                pe.wait_ge(hc_summed.sem, hc_summed.at(2 * DS + 4))
                pe.sem_inc(y_ready.sem, 1)
        for s in b_here:
            s.passed(LOOPS * 16)
        decay.passed(DS * CI)
        scanned.passed((DS + UN) * CI)
        dbu_ready.passed(DS)
        c_ready.passed(DS)
        if q + 1 < CPB:
            carried.passed(DS)
        hc_ready.passed(2 * DS + 4)
        hc_summed.passed(2 * DS + 4)
        y_ready.passed(1)
        gated.passed(CI)



SCORE_Q = (0, 0, 0, 1, 1, 1, 2)
SCORE_K = (0, 1, 2, 0, 1, 2, 0)
NSLOT = len(SCORE_Q)
MAX_ROW = NSLOT * DK


def split_heads(k, q, kk, nk, q8, k8, ctx):
    scale = 1.0 / DK ** 0.5
    qp = k.sb("q_split", [P, 3, C, T], BF16, ctx=ctx)
    kp = k.sb("k_split", [P, 3, C, nk], BF16, ctx=ctx)
    qr, kr = q, kk
    q_split, k_split = k.sig("q_split"), k.sig("k_split")
    slots_in = k.sig("slots_in")
    stored = [k.sig(f"part_stored{n}") for n in range(6)]
    with k.nc.Block() as block:
        @block.scalar
        def _(act):
            act.activation(qp[:, 0], q, ACT.Copy, scale=scale).then_inc(q_split.sem, 1)
            act.activation(kp[:, 0], kk, ACT.Copy).then_inc(k_split.sem, 1)
            act.wait_ge(q_split.sem, q_split.at(2))
            act.activation(qp[:, 1], qr, ACT.Copy).then_inc(q_split.sem, 1)
            act.wait_ge(k_split.sem, k_split.at(2))
            act.activation(kp[:, 1], kr, ACT.Copy).then_inc(k_split.sem, 1)

        @block.vector
        def _(dve):
            dve.wait_ge(q_split.sem, q_split.at(1))
            dve.scalar_tensor_tensor(qr, q, scale, qp[:, 0], ALU.mult, ALU.subtract).then_inc(q_split.sem, 1)
            dve.wait_ge(q_split.sem, q_split.at(3))
            dve.tensor_tensor(qp[:, 2], qr, qp[:, 1], ALU.subtract).then_inc(q_split.sem, 1)

        @block.gpsimd
        def _(pool):
            pool.wait_ge(k_split.sem, k_split.at(1))
            pool.tensor_tensor(kr, kk, kp[:, 0], ALU.subtract).then_inc(k_split.sem, 1)
            pool.wait_ge(k_split.sem, k_split.at(3))
            pool.tensor_tensor(kp[:, 2], kr, kp[:, 1], ALU.subtract).then_inc(k_split.sem, 1)

        @block.sync
        def _(sp):
            plan = ((q_split, qp, q8, k.q_parts, SCORE_Q, T), (k_split, kp, k8, k.k_parts, SCORE_K, nk))

            def store(n):
                part, (done, parts, _, dram, _, cols) = n // 2, plan[n % 2]
                sp.wait_ge(done.sem, done.at((1, 3, 4)[part]))
                sp.dma_start(dram[part, :, 0:cols].rearrange("(c p) t -> p c t", p=P), parts[:, part])\
                  .then_inc(stored[n].sem, 16)

            def fetch(n):
                part, (_, _, rows8, dram, slots, cols) = n // 2, plan[n % 2]
                sp.wait_ge(stored[n].sem, stored[n].at(16))
                for s in range(NSLOT):
                    if slots[s] == part:
                        sp.dma_start(rows8[s * DK:(s + 1) * DK, :, :],
                                     dram[part, :, 0:cols].rearrange("(h p) t -> p h t", p=DK)).then_inc(slots_in.sem, 16)

            store(0)
            store(1)
            zeros = k.zeros[0:3, :].bitcast(BF16)
            sp.dma_start(q8[MAX_ROW:MAX_ROW + 3, :, :].rearrange("p h t -> p (h t)").rearrange("p (a n) -> p a n", n=2 * D),
                         zeros.rearrange("p (a n) -> p a n", a=1).broadcast_to([3, H * T // (2 * D), 2 * D]))\
              .then_inc(slots_in.sem, 16)
            for n in range(6):
                fetch(n)
                if n + 2 < 6:
                    store(n + 2)
            sp.wait_ge(slots_in.sem, slots_in.at(16 * (2 * NSLOT + 1)))
    q_split.passed(4)
    k_split.passed(4)
    slots_in.passed(16 * (2 * NSLOT + 1))
    for s in stored:
        s.passed(16)


def slots(k, nk, ctx):
    q8 = k.sb("q8", [P, H, T], BF16, ctx=ctx)
    k8 = k.sb("k8", [P, H, nk], BF16, ctx=ctx)
    q_fill = (q8[96:P, :, :].bitcast(F32), 0.0)
    k_fill = (k8[96:P, :, :].bitcast(F32), TWO_ONES) if nk % 2 == 0 else (k8[96:P, :, :], 1.0)
    return q8, k8, q_fill, k_fill


def attention(k, q, kk, v, q8, k8, nk, causal, recip, wo, out, ctx):
    nc, ps = k.nc, k.ps
    KT = (nk + P - 1) // P
    negmax = k.sb("negmax", [P, T // P, H], ctx=ctx)
    with ExitStack() as c2:
        split_heads(k, q, kk, nk, q8, k8, c2)

    scored, maxed = k.sig("scored"), k.sig("maxed")
    turned, split = k.sig("turned"), k.sig("split")
    QT = T // P
    keys = [(t + 1) * P if causal else nk for t in range(QT)]
    RING = 4 if causal else 2
    ROOM = 8 // RING * W
    per = [ROOM // (W // 2 if n <= W // 2 else W if n <= W else 2 * W) for n in keys]
    before = [sum(H // p for p in per[:t]) for t in range(QT + 1)]
    swept, halved = k.sig("swept"), k.sig("halved")
    flat = ps[:, :, :].rearrange("p a b -> p (a b)")
    krows = min(P, nk)
    prob = k.sb("prob", [P, 4, 2, W], ctx=ctx)
    vh = k.sb("vh", [P, 2, 4, KT, 2 * DK], ctx=ctx)
    prepared = k.sig("prepared")
    max_ctx = ExitStack()
    rest = k.sb("max_rest", [H, T], ctx=max_ctx)
    mparts = k.sb("max_parts", [H, 3, T], BF16, ctx=max_ctx)
    if causal:
        sweep = kk.rearrange("p c n -> p (c n)").rearrange("p (g n) -> p g n", g=RING)
    with nc.Block() as block:
        @block.gpsimd
        def _(pool):
            pool.memset(vh[:], 1.0).then_inc(prepared.sem, 1)
            pool.wait_ge(prepared.sem, prepared.at(1))
            pool.memset(prob[64:P, :, :, :], 0.0).then_inc(prepared.sem, 1)
            pool.wait_ge(prepared.sem, prepared.at(2))

        @block.scalar
        def _(act):
            for t in range(QT):
                if causal:
                    n, hg = keys[t], per[t]
                    with act.Fori(0, H // hg // RING) as i:
                        for g in range(RING):
                            act.wait_ge(scored.sem, i * RING + scored.at(before[t] + g + 1))
                            act.wait_ge(maxed.sem, i * RING + maxed.at(before[t] + g + 1 - RING))
                            banks = flat[:, g * ROOM:(g + 1) * ROOM].rearrange("p (h n) -> p h n", h=hg)
                            act.activation(sweep[:, g, 0:hg * n // 2].rearrange("p (h n) -> p h n", h=hg),
                                           banks[:, :, n // 2:n], ACT.Copy).then_inc(halved.sem, 1)

        @block.tensor
        def _(pe):
            for t in range(QT):
                n, hg = keys[t], per[t]
                room = ROOM // hg
                with pe.Fori(0, H // hg // RING) as i:
                    for g in range(RING):
                        if causal:
                            pe.wait_ge(swept.sem, i * (RING * hg) + swept.at(H * t + (g + 1 - RING) * hg))
                        else:
                            pe.wait_ge(maxed.sem, i * RING + maxed.at(before[t] + g + 1 - RING))
                        for j in range(hg):
                            at, head = g * ROOM + j * room, bass.ds(i * (RING * hg) + g * hg + j, 1)
                            for o in range(0, n, W):
                                m = min(W, n - o)
                                mm = pe.matmul(flat[:, at + o:at + o + m], q8[:, head, t * P:(t + 1) * P],
                                               k8[:, head, o:o + m], start=True, stop=True)
                            if causal:
                                mm = pe.matmul(flat[:, at + n - P:at + n], k.ident16[:], k.late_key[:], start=False,
                                               stop=True, skip_group_check=True)
                        mm.then_inc(scored.sem, 1)
            pe.wait_ge(maxed.sem, maxed.at(before[QT]))
            for t in range(QT):
                mm = pe.transpose(flat[0:H, t * P:(t + 1) * P], negmax[:, t, :], k.ident[:])
            mm.then_inc(turned.sem, 1)

        @block.vector
        def _(dve):
            def reduce_group(i, g, t):
                n, hg = keys[t], per[t]
                banks = flat[:, g * ROOM:(g + 1) * ROOM].rearrange("p (h n) -> p h n", h=hg)
                dve.wait_ge(scored.sem, i * RING + scored.at(before[t] + g + 1))
                dve.tensor_reduce(negmax[:, t, bass.ds(i * (RING * hg) + g * hg, hg)], banks[:, :, 0:n], AX.X,
                                  ALU.max, negate=True).then_inc(maxed.sem, 1)

            def sweep_group(i, g, t):
                hg, half = per[t], keys[t] // 2
                dve.wait_ge(halved.sem, i * RING + halved.at(before[t] + g + 1))
                for j in range(hg):
                    at = g * ROOM + j * (ROOM // hg)
                    later = sweep[:, g, j * half:(j + 1) * half]
                    dve.tensor_tensor_scan(later, flat[:, at:at + half], later, -3e38, ALU.max, ALU.max).then_inc(swept.sem, 1)

            def last_of_sweep(i, g, t):
                hg, half = per[t], keys[t] // 2
                dve.wait_ge(swept.sem, i * (RING * hg) + swept.at(H * t + (g + 1) * hg))
                dve.tensor_scalar(negmax[:, t, bass.ds(i * (RING * hg) + g * hg, hg)],
                                  sweep[:, g, 0:hg * half].rearrange("p (h n) -> p h n", h=hg)[:, :, half - 1], -1.0, None,
                                  ALU.mult).then_inc(maxed.sem, 1)

            for t in range(QT):
                with dve.Fori(0, H // per[t] // RING) as i:
                    for g in range(RING):
                        if causal:
                            sweep_group(i, g, t)
                            if g:
                                last_of_sweep(i, g - 1, t)
                        else:
                            reduce_group(i, g, t)
                    if causal:
                        last_of_sweep(i, RING - 1, t)
            m = flat[0:H, 0:T]
            dve.wait_ge(turned.sem, turned.at(1))
            dve.tensor_copy(mparts[:, 0, :], m).then_inc(split.sem, 1)
            dve.wait_ge(split.sem, split.at(1))
            dve.tensor_tensor(rest[:], m, mparts[:, 0, :], ALU.subtract).then_inc(split.sem, 1)
            dve.wait_ge(split.sem, split.at(2))
            dve.tensor_copy(mparts[:, 1, :], rest[:]).then_inc(split.sem, 1)
            dve.wait_ge(split.sem, split.at(3))
            dve.tensor_tensor(mparts[:, 2, :], rest[:], mparts[:, 1, :], ALU.subtract).then_inc(split.sem, 1)

        @block.sync
        def _(sp):
            sp.wait_ge(split.sem, split.at(4))
            sp.dma_start(k.m_parts.rearrange("s h t -> h s t"), mparts[:]).then_inc(split.sem, 16)
            sp.wait_ge(split.sem, split.at(20))
            sp.dma_start(q8[MAX_ROW:MAX_ROW + 3, :, :], k.m_parts).then_inc(split.sem, 16)
            sp.wait_ge(split.sem, split.at(36))
    max_ctx.close()
    prepared.passed(2)
    if causal:
        swept.passed(H * QT)
        halved.passed(before[QT])
    scored.passed(before[QT])
    maxed.passed(before[QT])
    turned.passed(1)
    split.passed(36)

    fetched, attended = k.sig("fetched"), k.sig("attended")

    def fetch_sums(sp, qc):
        cols = slice(qc * W, (qc + 1) * W)
        for c in range(C):
            for to, which, first in ((q[:, c, cols], 0, 0), (recip[:, c, :], 1, DK)):
                rows = k.o_rows[2 * c:2 * c + 2, :, which, cols].rearrange("g (j d) t -> (g j) d t", j=4)
                sp.dma_start(to, rows[:, first:first + DK, :]).then_inc(fetched.sem, 16)

    def normalise(dve, qc):
        x = q[:, :, qc * W:(qc + 1) * W]
        dve.wait_ge(fetched.sem, fetched.at(16 * 2 * C))
        dve.tensor_tensor(x, x, recip[:], ALU.mult).then_inc(attended.sem, 1)

    with ExitStack() as c2:
        osb = k.sb("osb", [P, 2, 2, W], ctx=c2)
        score, weighed, used, v_ready = k.sig("score"), k.sig("weighed"), k.sig("used"), k.sig("v_ready")
        o_taken = k.sig("o_taken")
        stored = [k.sig("o_stored0"), k.sig("o_stored1")]
        for qc in range(CPB):
            tiles = [(t, max(0, t * P - qc * W)) for t in range(min(KT, (qc + 1) * W // P) if causal else KT)]
            nt = len(tiles)
            nsteps = 2 * nt
            npairs = 2 * nsteps

            def ago(m):
                return 3 if m >= 3 else npairs + m - max(x for x in range(npairs) if x % 3 == m)

            with nc.Block() as block:
                @block.gpsimd
                def _(pool):
                    with pool.Fori(0, H // 8) as i:
                        for g in range(2):
                            pool.wait_ge(used.sem, i * nsteps + used.at((g + 1) * nt - nsteps))
                            pool.tensor_copy(vh[:, g, :, :, 0:DK],
                                             v[:, :, bass.ds(i * (8 * DK) + g * 4 * DK, 4 * DK)]
                                             .rearrange("p t (j d) -> p j t d", j=4)).then_inc(v_ready.sem, 1)

                @block.tensor
                def _(pe):
                    with pe.Fori(0, H // 8) as i:
                        def scores(m):
                            s, p = divmod(m, 2)
                            g, (t, first) = s // nt, tiles[s % nt]
                            diag = causal and t * P >= qc * W
                            pe.wait_ge(weighed.sem, i * npairs + weighed.at(m + 1 - ago(m)))
                            for h in range(2):
                                head = bass.ds(i * 8 + 4 * g + 2 * p + h, 1)
                                bank = 2 * (m % 3) + h
                                mm = pe.matmul(ps[0:krows, bank, first:W], k8[:, head, t * P:t * P + krows],
                                               q8[:, head, qc * W + first:(qc + 1) * W], start=True, stop=True)
                                if diag:
                                    mm = pe.matmul(ps[:, bank, first:first + P], k.ident16[:], k.early_query[:],
                                                   start=False, stop=True, skip_group_check=True)
                            mm.then_inc(score.sem, 1)

                        def sums(s):
                            g, (t, first) = s // nt, tiles[s % nt]
                            pe.wait_ge(weighed.sem, i * npairs + weighed.at(2 * s + 2))
                            if s % nt == 0:
                                pe.wait_ge(v_ready.sem, i * 2 + v_ready.at(g + 1))
                                pe.wait_ge(o_taken.sem, i * 4 + o_taken.at(2 * g - 2))
                            for j in range(4):
                                mm = pe.matmul(ps[32 * j:32 * j + 32, 6 + g, first:W], vh[:, g, j, t, :],
                                               prob[:, (2 * s + j // 2) % 4, j % 2, first:W],
                                               start=(s % nt == 0), stop=(s % nt == nt - 1), skip_group_check=True)
                            mm.then_inc(used.sem, 1)

                        for m in range(3):
                            scores(m)
                        for s in range(nsteps):
                            for m in (2 * s + 3, 2 * s + 4):
                                if m == 2 * s + 4:
                                    sums(s)
                                if m < npairs:
                                    scores(m)

                @block.scalar
                def _(act):
                    with act.Fori(0, H // 8) as i:
                        for m in range(npairs):
                            first = tiles[m // 2 % nt][1]
                            act.wait_ge(score.sem, i * npairs + score.at(m + 1))
                            act.wait_ge(used.sem, i * nsteps + used.at(m // 2 - 1))
                            act.activation(prob[0:krows, m % 4, :, first:W],
                                           ps[0:krows, 2 * (m % 3):2 * (m % 3) + 2, first:W], ACT.Exp)\
                               .then_inc(weighed.sem, 1)

                @block.vector
                def _(dve):
                    if qc:
                        normalise(dve, qc - 1)
                    with dve.Fori(0, H // 8) as i:
                        for g in range(2):
                            dve.wait_ge(used.sem, i * nsteps + used.at((g + 1) * nt))
                            dve.wait_ge(stored[g].sem, i * 16 + stored[g].at(0))
                            dve.reciprocal(osb[:, g, 1, :], ps[:, 6 + g, :]).then_inc(o_taken.sem, 1)
                            dve.tensor_copy(osb[:, g, 0, :], ps[:, 6 + g, :]).then_inc(o_taken.sem, 1)

                @block.sync
                def _(sp):
                    if qc:
                        fetch_sums(sp, qc - 1)
                    with sp.Fori(0, H // 8) as i:
                        for g in range(2):
                            sp.wait_ge(o_taken.sem, i * 4 + o_taken.at(2 * g + 2))
                            sp.dma_start(k.o_rows[bass.ds(i * 2 + g, 1), :, :, qc * W:(qc + 1) * W]
                                         .rearrange("a p s t -> p (a s) t"), osb[:, g, :, :]).then_inc(stored[g].sem, 16)
                    for g in range(2):
                        sp.wait_ge(stored[g].sem, stored[g].at(H // 8 * 16))
            if qc:
                fetched.passed(16 * 2 * C)
                attended.passed(1)
            score.passed(H // 8 * npairs)
            weighed.passed(H // 8 * npairs)
            used.passed(H // 8 * nsteps)
            v_ready.passed(H // 4)
            o_taken.passed(H // 2)
            for s in stored:
                s.passed(H // 8 * 16)

    tiles = []
    for m in range(C):
        for h in range(CPB):
            prods = [(wo[:, c, m * P:(m + 1) * P], q[:, c, h * W:(h + 1) * W]) for c in range(C)]
            tiles.append(Tile(prods, "dve", add_bank(out[:, m, h * W:(h + 1) * W])))
    return Pending(lambda sp: fetch_sums(sp, CPB - 1), lambda dve: normalise(dve, CPB - 1), tiles, attended)


def add_bank(x):
    return lambda eng, bank: eng.tensor_tensor(x, x, bank, ALU.add)


def cross(k, a):
    X = k.X
    with ExitStack() as ctx:
        XN = k.sb("XN", [P, C, N], ctx=ctx)
        w = [k.sb(n, [P, C, D], ctx=ctx) for n in ("wq", "wk", "wv", "wo")]
        cx = k.sb("cx", [P, C, B * S2], ctx=ctx)
        q8, k8, q_rest, k_rest = slots(k, S2, ctx)
        norm(k, X, XN, loads=[(cx[:], a["ctx"])] + [(t[:], a["cross_" + n]) for t, n in zip(w, "qkvo")],
             fills=[q_rest, k_rest])
        qs = [k.sb("q", [P, C, T], ctx=ctx) for b in range(B)]
        recip = k.sb("recip", [P, C, W], ctx=ctx)
        pending = None
        for b in range(B):
            q = qs[b]
            with ExitStack() as c2:
                kk = k.sb("kk", [P, C, S2], ctx=c2)
                v = k.sb("v", [P, 1, D], ctx=c2)
                steps(k, "chain", [("dve", lambda e: e.memset(v[:], 0.0))])
                tiles = []
                for m in range(C):
                    cols = slice(m * P, (m + 1) * P)
                    for h in range(CPB):
                        prods = [(w[0][:, c, cols], XN[:, c, b * T + h * W:b * T + (h + 1) * W]) for c in range(C)]
                        tiles.append(Tile(prods, "act", copy_to(q[:, m, h * W:(h + 1) * W])))
                    prods = [(w[1][:, c, cols], cx[:, c, b * S2:(b + 1) * S2]) for c in range(C)]
                    tiles.append(Tile(prods, "dve", dve_copy_to(kk[:, m, :]), cols=S2))
                prods = [(cx[:, c, b * S2:(b + 1) * S2], w[2][:, c, :]) for c in range(C)]
                tiles.append(Tile(prods, "dve", dve_copy_to(v[0:S2, 0, :]), rows=S2, cols=D))
                project(k, tiles, pending=pending)
                pending = attention(k, q[:], kk[:], v, q8, k8, S2, False, recip, w[3], X[:, :, b * T:(b + 1) * T], c2)
        project(k, [], pending=pending)



def decoder(k, a):
    X = k.X
    with ExitStack() as ctx:
        H2 = k.sb("H2", [P, C, N], ctx=ctx)
        vec = k.sb("ffn_vec", [P, C, 4 + TAPS], ctx=ctx)
        with ExitStack() as c1:
            q8, k8, q_rest, k_rest = slots(k, T, c1)
            norm(k, X, H2, loads=[(vec[:], a["ffn_vec"])], fills=[q_rest])
            HN = k.sb("HN", [P, C, N], ctx=c1)
            w = k.sb("w_attn", [P, C, 5 * D], ctx=c1)
            wo = k.sb("w_proj", [P, C, D], ctx=c1)
            rope = k.sb("rope", [P, 2, T], ctx=c1)
            norm(k, H2, HN, weight=vec[:, :, 0], bias=vec[:, :, 1],
                 loads=[(w[:], a["ffn_attn"]), (wo[:], a["ffn_proj"]), (rope[:], a["rope"])], fills=[k_rest])
            qs = [k.sb("q", [P, C, T], ctx=c1) for b in range(B)]
            recip = k.sb("recip", [P, C, W], ctx=c1)
            pending = None
            for b in range(B):
                with ExitStack() as c2:
                    pending = causal_batch(k, b, HN, H2, vec, w, wo, rope, qs[b], q8, k8, recip, pending, c2)
            project(k, [], pending=pending)
        experts(k, a, H2, vec)


def causal_batch(k, b, HN, H2, vec, w, wo, rope, q, q8, k8, recip, pending, ctx):
    kk = k.sb("kk", [P, C, T], ctx=ctx)
    v = k.sb("v", [P, T // P, D], ctx=ctx)
    with ExitStack() as c2:
        hc = k.sb("hc", [P, C, T], ctx=c2)
        turned = k.sb("turned_qk", [P, 2, C, T], ctx=c2)
        ops = []
        for c in range(C):
            x = HN[:, c, b * T:(b + 1) * T]
            ops.append(("dve", lambda e, c=c, x=x: e.tensor_scalar(hc[:, c, :], x, vec[:, c, 6:7], None, ALU.mult)))
            for d in (1, 2):
                ops.append(("dve", lambda e, c=c, x=x, d=d: e.scalar_tensor_tensor(
                    hc[:, c, d:T], x[:, 0:T - d], vec[:, c, 6 - d:7 - d], hc[:, c, d:T], ALU.mult, ALU.add)))
        steps(k, "chain", ops)
        tiles = []
        for h in range(CPB):
            cols = slice(h * W, (h + 1) * W)
            for n, (dst, table) in enumerate(((q, 0), (turned[:, 0], 1), (kk, 0), (turned[:, 1], 1))):
                for m in range(C):
                    prods = [(w[:, c, n * D + m * P:n * D + (m + 1) * P], hc[:, c, cols]) for c in range(C)]
                    tiles.append(Tile(prods, "dve", lambda e, bank, dst=dst, m=m, table=table, cols=cols:
                                      e.tensor_tensor(dst[:, m, cols], bank, rope[:, table, cols], ALU.mult)))
            for t in range(4 * h, 4 * h + 4):
                prods = [(hc[:, c, t * P:(t + 1) * P], w[:, c, 4 * D:5 * D]) for c in range(C)]
                tiles.append(Tile(prods, "act", copy_to(v[:, t, :]), cols=D))
        project(k, tiles, pending=pending)
        steps(k, "chain", [("dve", lambda e: e.tensor_tensor(q[:], q[:], turned[:, 0], ALU.add)),
                           ("pool", lambda e: e.tensor_tensor(kk[:], kk[:], turned[:, 1], ALU.add))])
    return attention(k, q[:], kk[:], v, q8, k8, T, True, recip, wo, H2[:, :, b * T:(b + 1) * T], ctx)


def experts(k, a, H2, vec):
    nc, ps, X = k.nc, k.ps, k.X
    FT = FF // P
    TT = N // P
    NT = TT + E_ - 1
    with ExitStack() as ctx:
        wv = k.sb("w_wv", [P, E_ * C * 2 * FF], ctx=ctx)
        wp = k.sb("w_down", [P, E_ * FT * D], ctx=ctx)
        HN = k.sb("HN", [P, C, N], ctx=ctx)
        rows = k.sb("rows", [P, TT, D], ctx=ctx)
        wr = k.sb("w_router", [P, C, E_], ctx=ctx)
        before = k.sb("before", [P, P], ctx=ctx)
        counts = k.sb("tile_counts", [P, TT + NT], ctx=ctx)
        slot = k.sb("slot", [P, TT], I32, ctx=ctx)
        expert = k.sb("tile_expert", [1, NT + 1], I32, ctx=ctx)
        xs = k.xs.rearrange("(s p) d -> p s d", p=P)
        weights_in = k.sig("weights_in")
        norm(k, H2, HN, weight=vec[:, :, 2], bias=vec[:, :, 3],
             loads=[(wr[:], a["router"]), (before[:], a["before"]), (counts[:], a["tile_counts"]),
                    (xs, k.zeros[:].rearrange("p (a d) -> p a d", a=1).broadcast_to([P, NT, D]))],
             later=[(wv[:], a["expert_wv"]), (wp[:], a["expert_proj"])], later_in=weights_in)
        sort_tokens(k, X, H2, HN, wr, before, counts, rows, slot, expert)
        with ExitStack() as c2:
            run_tiles(k, wv, wp, rows, slot, expert, weights_in, NT, c2)
        weights_in.passed(32)

        gathered = [k.sig(f"gathered{h}") for h in range(NCH)]
        turned, added = k.sig("turned"), k.sig("added")
        with nc.Block() as block:
            @block.gpsimd
            def _(pool):
                for t in range(TT):
                    pool.indirect_dma_start(rows[:, t, :], None, k.ys,
                                            bass.IndirectOffsetOnAxis(ap=slot[:, t:t + 1], axis=0))\
                        .then_inc(gathered[t * P // W].sem, 16)

            @block.tensor
            def _(pe):
                for h in range(NCH):
                    pe.wait_ge(gathered[h].sem, gathered[h].at(16 * W // P))
                    for t in range(W // P):
                        for c in range(C):
                            mm = pe.transpose(ps[:, 2 * h + c, t * P:(t + 1) * P],
                                              rows[:, h * (W // P) + t, c * P:(c + 1) * P], k.ident[:])
                    mm.then_inc(turned.sem, 1)

            @block.vector
            def _(dve):
                for h in range(NCH):
                    dve.wait_ge(turned.sem, turned.at(h + 1))
                    x = X[:, :, h * W:(h + 1) * W]
                    dve.tensor_tensor(x, x, ps[:, 2 * h:2 * h + 2, :], ALU.add).then_inc(added.sem, 1)
        for s in gathered:
            s.passed(16 * W // P)
        turned.passed(NCH)
        added.passed(NCH)


def sort_tokens(k, X, H2, HN, wr, before, counts, rows, slot, expert):
    nc, ps = k.nc, k.ps
    TT = N // P
    NT = TT + E_ - 1
    with ExitStack() as ctx:
        best = k.sb("best", [P, TT], ctx=ctx)
        free = k.sb("free", [P, TT], ctx=ctx)
        pick = k.sb("pick", [P, TT, E_], ctx=ctx)
        ones = k.sb("ones", [P, P], ctx=ctx)
        upto = k.sb("upto", [P, E_, TT], ctx=ctx)
        over = k.sb("over", [P, E_, TT], ctx=ctx)
        tiles_of = k.sb("tiles_of", [P, E_], ctx=ctx)
        tiles_upto = k.sb("tiles_upto", [P, E_], ctx=ctx)
        place = k.sb("place", [P, E_, TT], ctx=ctx)
        slot_f = k.sb("slot_f", [P, TT], ctx=ctx)
        past = k.sb("past", [1, NT, E_ - 1], ctx=ctx)
        expert_f = k.sb("expert_f", [1, NT], ctx=ctx)
        logits_ready, picked, counted = k.sig("logits_ready"), k.sig("picked"), k.sig("counted")
        turned, rows_in, sorting, added = k.sig("turned"), k.sig("rows_in"), k.sig("sorting"), k.sig("added")
        logits = ps[:, 0, 0:TT * E_].rearrange("p (t e) -> p t e", e=E_)
        rank = ps[:, 1, 0:TT * E_].rearrange("p (t e) -> p e t", e=E_)
        total = ps[:, 1, TT * E_:2 * TT * E_].rearrange("p (t e) -> p e t", e=E_)
        steps_taken = 0
        with nc.Block() as block:
            @block.tensor
            def _(pe):
                for t in range(TT):
                    for c in range(C):
                        mm = pe.matmul(logits[:, t, :], HN[:, c, t * P:(t + 1) * P], wr[:, c, :],
                                       start=(c == 0), stop=(c == C - 1))
                mm.then_inc(logits_ready.sem, 1)

                def turn(g):
                    if g >= 6:
                        pe.wait_ge(rows_in.sem, rows_in.at(g - 5))
                    for t in (2 * g, 2 * g + 1):
                        for c in range(C):
                            mm = pe.transpose(ps[:, 2 + g % 6, (t % 2) * D + c * P:(t % 2) * D + (c + 1) * P],
                                              HN[:, c, t * P:(t + 1) * P], k.ident[:])
                    mm.then_inc(turned.sem, 1)

                for g in range(TT // 2):
                    turn(g)
                pe.wait_ge(picked.sem, picked.at(1))
                flat = pick[:].rearrange("p t e -> p (t e)")
                pe.matmul(ps[:, 1, 0:TT * E_], before[:], flat, start=True, stop=True)
                pe.matmul(ps[:, 1, TT * E_:2 * TT * E_], ones[:], flat, start=True, stop=True).then_inc(counted.sem, 1)

            @block.scalar
            def _(act):
                for g in range(TT // 2):
                    act.wait_ge(turned.sem, turned.at(g + 1))
                    act.activation(rows[:, 2 * g:2 * g + 2, :], ps[:, 2 + g % 6, :].rearrange("p (t d) -> p t d", t=2),
                                   ACT.Copy).then_inc(rows_in.sem, 1)

            @block.gpsimd
            def _(pool):
                pool.tensor_tensor(X[:], X[:], H2[:], ALU.add).then_inc(added.sem, 1)
                pool.wait_ge(added.sem, added.at(1))

            @block.vector
            def _(dve):
                nonlocal steps_taken

                def step(instruction):
                    nonlocal steps_taken
                    steps_taken += 1
                    instruction.then_inc(sorting.sem, 1)
                    dve.wait_ge(sorting.sem, sorting.at(steps_taken))

                def by(ap, shape, pattern, **kw):
                    return ap.rearrange(pattern, **kw).broadcast_to(shape)

                dve.memset(ones[:], 1.0).then_inc(sorting.sem, 1)
                dve.memset(free[:], 1.0).then_inc(sorting.sem, 1)
                steps_taken += 2
                dve.wait_ge(logits_ready.sem, logits_ready.at(1))
                step(dve.tensor_reduce(best[:], logits, AX.X, ALU.max))
                step(dve.tensor_tensor(pick[:], logits, by(best[:], [P, TT, E_], "p (t a) -> p t a", a=1), ALU.is_ge))
                for x in range(1, E_):
                    step(dve.tensor_tensor(free[:], free[:], pick[:, :, x - 1], ALU.subtract))
                    last = dve.tensor_tensor(pick[:, :, x], pick[:, :, x], free[:], ALU.mult)
                    if x < E_ - 1:
                        step(last)
                last.then_inc(picked.sem, 1)
                dve.wait_ge(counted.sem, counted.at(1))
                for e in range(E_):
                    scan = dve.tensor_tensor_scan(upto[:, e, :], ones[:, 0:TT], total[:, e, :], 0.0, ALU.mult, ALU.add)
                    step(scan)
                step(dve.tensor_tensor(over[:], upto[:, :, TT - 1:TT].broadcast_to([P, E_, TT]),
                                       by(counts[:, 0:TT], [P, E_, TT], "p (a t) -> p a t", a=1), ALU.is_gt))
                step(dve.tensor_reduce(tiles_of[:], over[:], AX.X, ALU.add))
                step(dve.tensor_tensor_scan(tiles_upto[:], ones[:, 0:E_], tiles_of[:], 0.0, ALU.mult, ALU.add))
                step(dve.tensor_tensor(past[:], by(counts[0:1, TT:TT + NT], [1, NT, E_ - 1], "p (s a) -> p s a", a=1),
                                       by(tiles_upto[0:1, 0:E_ - 1], [1, NT, E_ - 1], "p (a e) -> p a e", a=1),
                                       ALU.is_ge))
                step(dve.tensor_reduce(expert_f[:], past[:], AX.X, ALU.add))
                step(dve.tensor_copy(expert[0:1, 0:NT], expert_f[:]))
                step(dve.tensor_tensor(tiles_upto[:], tiles_upto[:], tiles_of[:], ALU.subtract))
                step(dve.tensor_tensor(place[:], upto[:], total, ALU.subtract))
                step(dve.tensor_tensor(place[:], place[:], rank, ALU.add))
                step(dve.scalar_tensor_tensor(place[:], by(tiles_upto[:], [P, E_, TT], "p (e a) -> p e a", a=1),
                                              float(P), place[:], ALU.mult, ALU.add))
                step(dve.tensor_tensor(place[:], place[:], pick[:].rearrange("p t e -> p e t"), ALU.mult))
                step(dve.tensor_reduce(slot_f[:], place[:].rearrange("p e t -> p t e"), AX.X, ALU.add))
                step(dve.tensor_copy(slot[:], slot_f[:]))
        for s in (logits_ready, picked, counted, added):
            s.passed(1)
        turned.passed(TT // 2)
        rows_in.passed(TT // 2)
        sorting.passed(steps_taken)


class Beat:

    def __init__(self, i, c):
        self.i, self.c = i, c

    def times(self, per, extra=0):
        return per * self.c + extra if self.i is None else self.i * (2 * per) + (per * self.c + extra)

    def wait(self, eng, signal, per, extra):
        if self.i is not None or per * self.c + extra > 0:
            eng.wait_ge(signal.sem, self.times(per, signal.base + extra))

    def next(self, n=1):
        return Beat(self.i, self.c + n)


def run_tiles(k, wv, wp, rows, slot, expert, weights_in, NT, ctx):
    nc, ps = k.nc, k.ps
    FT = FF // P
    HALF = FF // 2
    HT = FT // 2
    xrow = k.sb("x_rows", [P, 2, D], ctx=ctx)
    xt = k.sb("x_turned", [P, 2, C, P], ctx=ctx)
    gate = k.sb("gate", [P, 2, HALF], ctx=ctx)
    hid = k.sb("hid", [P, 2, HALF], ctx=ctx)
    hid_t = k.sb("hid_turned", [P, 2, HT, P], ctx=ctx)
    yrow = k.sb("y_rows", [P, 2, D], ctx=ctx)
    scattered = k.sig("scattered")
    x_here = [k.sig("x_here0"), k.sig("x_here1")]
    y_stored = [k.sig("y_stored0"), k.sig("y_stored1")]
    x_turned, x_copied = k.sig("x_turned"), k.sig("x_copied")
    pair, gated, hidden = k.sig("pair"), k.sig("gated"), k.sig("hidden")
    hid_turned, hid_copied, down = k.sig("hid_turned"), k.sig("hid_copied"), k.sig("down")
    y_copied = k.sig("y_copied")
    HID, OUT, XT = 4, 6, 7
    FIRST = 3
    LOOPS = (NT - FIRST - 1) // 2

    def all_tiles(eng, body):
        for c in range(FIRST):
            body(Beat(None, c), c % 2)
        with eng.Fori(0, LOOPS) as i:
            for c in range(FIRST, FIRST + 2):
                body(Beat(i, c), c % 2)
        for c in range(FIRST + 2 * LOOPS, NT):
            body(Beat(None, c), c % 2)

    with nc.Block() as block:
        @block.gpsimd
        def _(pool):
            for t in range(N // P):
                pool.indirect_dma_start(k.xs, bass.IndirectOffsetOnAxis(ap=slot[:, t:t + 1], axis=0),
                                        rows[:, t, :], None).then_inc(scattered.sem, 16)

        @block.sync
        def _(sp):
            def body(tile, p):
                tile.wait(sp, x_turned, 1, -1)
                sp.dma_start(xrow[:, p, :], k.xs[bass.ds(tile.times(P), P), :]).then_inc(x_here[p].sem, 16)
                if tile.i is not None or tile.c >= 2:
                    store(tile.next(-2), p)

            def store(tile, p):
                tile.wait(sp, y_copied, 1, 1)
                sp.dma_start(k.ys[bass.ds(tile.times(P), P), :], yrow[:, p, :]).then_inc(y_stored[p].sem, 16)

            sp.wait_ge(scattered.sem, scattered.at(16 * (N // P)))
            all_tiles(sp, body)
            for c in (NT - 2, NT - 1):
                store(Beat(None, c), c % 2)
            for p in range(2):
                sp.wait_ge(y_stored[p].sem, y_stored[p].at(16 * ((NT + 1 - p) // 2)))

        @block.tensor
        def _(pe):
            def turn_x(tile, p):
                tile.wait(pe, x_here[p], 8, 16 - 8 * p)
                for c in range(C):
                    mm = pe.transpose(ps[:, XT, p * D + c * P:p * D + (c + 1) * P], xrow[:, p, c * P:(c + 1) * P],
                                      k.ident[:])
                mm.then_inc(x_turned.sem, 1)

            def gate_value(tile, p, h, e):
                if h == 0:
                    tile.wait(pe, x_copied, 1, 1)
                tile.wait(pe, hidden, 2, h - 1)
                for g in range(2):
                    for c in range(C):
                        mm = pe.matmul(ps[:, 2 * h + g, :], xt[:, p, c, :],
                                       wv[:, bass.ds(e * (C * 2 * FF) + (c * 2 * FF + g * FF + h * HALF), HALF)],
                                       start=(c == 0), stop=(c == C - 1))
                mm.then_inc(pair.sem, 1)

            def turn_hidden(tile, h):
                tile.wait(pe, hidden, 2, h + 1)
                for f in range(HT):
                    mm = pe.transpose(ps[:, HID + h, f * P:(f + 1) * P], hid[:, h, f * P:(f + 1) * P], k.ident[:])
                mm.then_inc(hid_turned.sem, 1)

            def down_half(tile, h, e):
                tile.wait(pe, hid_copied, 2, h + 1)
                if h == 0:
                    tile.wait(pe, y_copied, 1, 0)
                for f in range(HT):
                    mm = pe.matmul(ps[:, OUT, 0:D], hid_t[:, h, f, :],
                                   wp[:, bass.ds(e * (FT * D) + (h * HT + f) * D, D)],
                                   start=(h == 0 and f == 0), stop=(h == 1 and f == HT - 1), skip_group_check=True)
                mm.then_inc(down.sem, 1)

            def experts_of(tile, n):
                return [pe.value_load(expert[0:1, bass.ds(tile.times(1, j), 1)], min_val=0, max_val=E_ - 1)
                        for j in range(n)]

            def body(tile, p, before, now, after):
                gate_value(tile, p, 1, now)
                if before is not None:
                    down_half(tile.next(-1), 1, before)
                turn_hidden(tile, 0)
                if after is not None:
                    turn_x(tile.next(), 1 - p)
                    gate_value(tile.next(), 1 - p, 0, after)
                down_half(tile, 0, now)
                turn_hidden(tile, 1)

            pe.wait_ge(weights_in.sem, weights_in.at(32))
            first = Beat(None, 0)
            e = experts_of(first, FIRST + 1)
            turn_x(first, 0)
            gate_value(first, 0, 0, e[0])
            for c in range(FIRST):
                body(Beat(None, c), c % 2, e[c - 1] if c else None, e[c], e[c + 1])
            with pe.Fori(0, LOOPS) as i:
                e = experts_of(Beat(i, FIRST - 1), 4)
                for c in range(2):
                    body(Beat(i, FIRST + c), (FIRST + c) % 2, e[c], e[c + 1], e[c + 2])
            rest = FIRST + 2 * LOOPS
            e = experts_of(Beat(None, rest - 1), NT - rest + 1)
            for c in range(rest, NT):
                body(Beat(None, c), c % 2, e[c - rest], e[c - rest + 1], e[c - rest + 2] if c + 1 < NT else None)
            down_half(Beat(None, NT - 1), 1, e[NT - rest])

        @block.scalar
        def _(act):
            def copy_x(tile, p):
                tile.wait(act, x_turned, 1, 1)
                tile.wait(act, pair, 2, -2)
                act.activation(xt[:, p, :, :], ps[:, XT, p * D:(p + 1) * D].rearrange("p (c n) -> p c n", c=C), ACT.Copy)\
                   .then_inc(x_copied.sem, 1)

            def silu(tile, h):
                tile.wait(act, pair, 2, h + 1)
                tile.wait(act, hidden, 2, h - 1)
                act.activation(gate[:, h, :], ps[:, 2 * h, :], ACT.Silu).then_inc(gated.sem, 1)

            def copy_y(tile, p):
                tile.wait(act, down, 2, 2)
                tile.wait(act, y_stored[p], 8, -8 * p)
                act.activation(yrow[:, p, :], ps[:, OUT, 0:D], ACT.Copy).then_inc(y_copied.sem, 1)

            def body(tile, p):
                silu(tile, 1)
                if tile.i is not None or tile.c >= 1:
                    copy_y(tile.next(-1), 1 - p)
                if tile.i is not None or tile.c + 1 < NT:
                    copy_x(tile.next(), 1 - p)
                    silu(tile.next(), 0)

            copy_x(Beat(None, 0), 0)
            silu(Beat(None, 0), 0)
            all_tiles(act, body)
            copy_y(Beat(None, NT - 1), (NT - 1) % 2)

        @block.vector
        def _(dve):
            def body(tile, p):
                for h in range(2):
                    tile.wait(dve, gated, 2, h + 1)
                    tile.wait(dve, hid_turned, 2, h - 1)
                    dve.tensor_tensor(hid[:, h, :], gate[:, h, :], ps[:, 2 * h + 1, :], ALU.mult)\
                       .then_inc(hidden.sem, 1)
                    tile.wait(dve, hid_turned, 2, h + 1)
                    tile.wait(dve, down, 2, h - 1)
                    dve.tensor_scalar(hid_t[:, h, :, :], ps[:, HID + h, :].rearrange("p (f n) -> p f n", f=HT),
                                      1.0, None, ALU.mult).then_inc(hid_copied.sem, 1)

            all_tiles(dve, body)
    scattered.passed(16 * (N // P))
    for p in range(2):
        x_here[p].passed(16 * ((NT + 1 - p) // 2))
        y_stored[p].passed(16 * ((NT + 1 - p) // 2))
    for s in (x_turned, x_copied, y_copied):
        s.passed(NT)
    for s in (pair, gated, hidden, hid_turned, hid_copied, down):
        s.passed(2 * NT)



def linear(k, a):
    nc, ps, X = k.nc, k.ps, k.X
    with ExitStack() as ctx:
        XN = k.sb("XN", [P, C, N], ctx=ctx)
        w = k.sb("w_qkv", [P, C, 3 * D], ctx=ctx)
        wo = k.sb("w_lproj", [P, C, D], ctx=ctx)
        bias = k.sb("lbias", [P, C], ctx=ctx)
        same = k.sb("same_head", [P, P], ctx=ctx)
        norm(k, X, XN, loads=[(w[:], a["lin_qkv"]), (wo[:], a["lin_proj"]), (bias[:], a["lin_bias"]),
                              (same[:], a["same_head"])])
        q = k.sb("lq", [P, C, N], ctx=ctx)
        o = k.sb("lo", [P, C, N], ctx=ctx)
        kt = k.sb("lk", [P, N // P, D + 1], ctx=ctx)
        vt = k.sb("lv", [P, N // P, D], ctx=ctx)
        tiles = []
        for t in range(N // P):
            prods = [(XN[:, c, t * P:(t + 1) * P], w[:, c, D:3 * D]) for c in range(C)]
            tiles.append(Tile(prods, "act", lambda e, bank, t=t: e.activation(kt[:, t, 0:D], bank[:, 0:D], ACT.Relu)))
            tiles.append(Tile([(XN[:, c, t * P:(t + 1) * P], w[:, c, 2 * D:3 * D]) for c in range(C)], "dve",
                              dve_copy_to(vt[:, t, :]), cols=D))
            tiles[-2].cols = D
            tiles[-2].products = [(l, r[:, 0:D]) for l, r in prods]
        for h in range(NCH):
            for m in range(C):
                prods = [(w[:, c, m * P:(m + 1) * P], XN[:, c, h * W:(h + 1) * W]) for c in range(C)]
                tiles.append(Tile(prods, "act", copy_to(q[:, m, h * W:(h + 1) * W], ACT.Relu)))
        project(k, tiles)
        ctxw = k.sb("ctxw", [P, B, C, P], ctx=ctx)
        ksw = k.sb("ksw", [P, B, C, P], ctx=ctx)
        ones = k.sb("lones", [P, P], ctx=ctx)
        steps(k, "chain", [("dve", lambda e: e.memset(ones[:], 1.0))])
        tiles = []
        for b in range(B):
            for c in range(C):
                tok = range(b * T // P, (b + 1) * T // P)
                kc = slice(c * P, (c + 1) * P)
                for dst, right in ((ctxw, [vt[:, t, kc] for t in tok]), (ksw, [ones[:] for t in tok])):
                    tiles.append(Tile([(kt[:, t, kc], r) for t, r in zip(tok, right)], "dve",
                                      lambda e, bank, dst=dst, b=b, c=c: e.tensor_tensor(dst[:, b, c, :], bank, same[:],
                                                                                         ALU.mult), cols=P))
        project(k, tiles)
        r0 = k.sb("root", [P, 2, W], ctx=ctx)
        r0sq = k.sb("root_sq", [P, 2, W], ctx=ctx)
        recip = k.sb("recip", [P, 2, W], ctx=ctx)
        summed, root, root_sq = k.sig("lin_summed"), k.sig("lin_root"), k.sig("lin_root_sq")
        newton, attended = k.sig("lin_newton"), k.sig("lin_attended")
        projected, added = k.sig("lin_projected"), k.sig("lin_added")
        SUM, Z, OUT = 0, 2, 4
        NT = NCH * C
        with nc.Block() as block:
            @block.tensor
            def _(pe):
                def products(n):
                    h, c = divmod(n, C)
                    cols = slice(h * W, (h + 1) * W)
                    if n >= 2:
                        pe.wait_ge(attended.sem, attended.at(n - 1))
                    pe.matmul(ps[:, Z + n % 2, :], ksw[:, h // CPB, c, :], q[:, c, cols], start=True, stop=True)
                    pe.matmul(ps[:, SUM + n % 2, :], ctxw[:, h // CPB, c, :], q[:, c, cols], start=True, stop=True)\
                      .then_inc(summed.sem, 1)

                def project_out(h):
                    pe.wait_ge(attended.sem, attended.at((h + 1) * C))
                    if h >= 2:
                        pe.wait_ge(added.sem, added.at((h - 1) * C))
                    for m in range(C):
                        for c in range(C):
                            mm = pe.matmul(ps[:, OUT + (h % 2) * C + m, :], wo[:, c, m * P:(m + 1) * P],
                                           o[:, c, h * W:(h + 1) * W], start=(c == 0), stop=(c == C - 1))
                        mm.then_inc(projected.sem, 1)

                for n in range(NT):
                    products(n)
                    if n % C == C - 1 and n > C:
                        project_out(n // C - 1)
                project_out(NCH - 1)

            @block.scalar
            def _(act):
                for n in range(NT):
                    act.wait_ge(summed.sem, summed.at(n + 1))
                    if n >= 2:
                        act.wait_ge(attended.sem, attended.at(n - 1))
                    act.activation(r0[:, n % 2, :], ps[:, Z + n % 2, :], ACT.Abs_reciprocal_sqrt,
                                   bias=k.eps[:, 1:2]).then_inc(root.sem, 1)
                    act.wait_ge(root.sem, root.at(n + 1))
                    act.activation(r0sq[:, n % 2, :], r0[:, n % 2, :], ACT.Square).then_inc(root_sq.sem, 1)

            @block.vector
            def _(dve):
                def attend(n):
                    h, c = divmod(n, C)
                    dve.wait_ge(root_sq.sem, root_sq.at(n + 1))
                    r, x = r0sq[:, n % 2, :], recip[:, n % 2, :]
                    dve.scalar_tensor_tensor(x, ps[:, Z + n % 2, :], EPS_F32, r, ALU.add, ALU.mult).then_inc(newton.sem, 1)
                    dve.wait_ge(newton.sem, newton.at(2 * n + 1))
                    dve.scalar_tensor_tensor(x, x, 2.0, r, ALU.subtract, ALU.mult).then_inc(newton.sem, 1)
                    dve.wait_ge(newton.sem, newton.at(2 * n + 2))
                    dve.scalar_tensor_tensor(o[:, c, h * W:(h + 1) * W], x, -1.0, ps[:, SUM + n % 2, :],
                                             ALU.mult, ALU.mult).then_inc(attended.sem, 1)

                def add(h):
                    for m in range(C):
                        x = X[:, m, h * W:(h + 1) * W]
                        dve.wait_ge(projected.sem, projected.at(h * C + m + 1))
                        dve.scalar_tensor_tensor(x, ps[:, OUT + (h % 2) * C + m, :], bias[:, m:m + 1], x,
                                                 ALU.add, ALU.add).then_inc(added.sem, 1)

                for n in range(NT):
                    attend(n)
                    if n % C == C - 1 and n > C:
                        add(n // C - 1)
                add(NCH - 1)
        for s in (summed, root, root_sq, attended, projected, added):
            s.passed(NT)
        newton.passed(2 * NT)


def cross_one(k, a):
    nc, ps, X = k.nc, k.ps, k.X
    G = W // P
    with ExitStack() as ctx:
        XN = k.sb("XN", [P, C, N], ctx=ctx)
        w = k.sb("w_one", [P, C, D], ctx=ctx)
        bias = k.sb("one_bias", [P, C], ctx=ctx)
        cx = k.sb("cx", [P, C, B * S2], ctx=ctx)
        ct = k.sb("ct", [P, B, D], ctx=ctx)
        mask_in = k.sb("mask_in", [P, B, S2], I32, ctx=ctx)
        mask = k.sb("mask", [P, B, S2], ctx=ctx)
        steps(k, "chain", [("dve", lambda e: e.memset(ct[:], 0.0))])
        norm(k, X, XN, loads=[(w[:], a["one_w"]), (bias[:], a["one_bias"]), (cx[:], a["ctx"]),
                              (ct[0:S2, :, :], a["ctx_rows"])]
             + [(mask_in[:, b, :], a["mask"][b:b + 1, :].broadcast_to([P, S2])) for b in range(B)])
        yp = k.sb("yp", [P, C, B * S2], ctx=ctx)
        xp = k.sb("xp", [P, C, N], ctx=ctx)
        steps(k, "chain", [("dve", lambda e: e.tensor_copy(mask[:], mask_in[:])),
                           ("dve", lambda e: e.tensor_scalar(mask[:], mask[:], -3e38, 10.0, ALU.mult, ALU.mult))])
        tiles = []
        for m in range(C):
            relu = lambda dst, m: (lambda e, bank: e.activation(dst, bank, ACT.Relu, bias=bias[:, m:m + 1]))
            tiles.append(Tile([(w[:, c, m * P:(m + 1) * P], cx[:, c, :]) for c in range(C)], "act",
                              relu(yp[:, m, :], m), cols=B * S2))
            for h in range(NCH):
                prods = [(w[:, c, m * P:(m + 1) * P], XN[:, c, h * W:(h + 1) * W]) for c in range(C)]
                tiles.append(Tile(prods, "act", relu(xp[:, m, h * W:(h + 1) * W], m)))
        project(k, tiles)
        sc = k.sb("sc", [P, NCH, G, S2], ctx=ctx)
        top = k.sb("top", [P, NCH, G], ctx=ctx)
        pt = k.sb("pt", [P, NCH, W], ctx=ctx)
        tiles = []
        for h in range(NCH):
            b = h // CPB
            for g in range(G):
                t = h * G + g
                prods = [(xp[:, c, t * P:(t + 1) * P], yp[:, c, b * S2:(b + 1) * S2]) for c in range(C)]
                tiles.append(Tile(prods, "dve", lambda e, bank, b=b, h=h, g=g: e.tensor_tensor(
                    sc[:, h, g, :], bank, mask[:, b, :], ALU.add), cols=S2))
        project(k, tiles)
        flat = sc[:].rearrange("p h g s -> p (h g) s")
        tflat = top[:].rearrange("p h g -> p (h g)")
        tb = top[:].rearrange("p h (g a) -> p (h g) a", a=1).broadcast_to([P, NCH * G, S2])
        steps(k, "chain", [("dve", lambda e: e.tensor_reduce(tflat, flat, AX.X, ALU.max)),
                           ("dve", lambda e: e.tensor_tensor(flat, flat, tb, ALU.subtract)),
                           ("act", lambda e: e.activation(flat, flat, ACT.Exp)),
                           ("dve", lambda e: e.tensor_reduce(tflat, flat, AX.X, ALU.add)),
                           ("dve", lambda e: e.reciprocal(tflat, tflat)),
                           ("dve", lambda e: e.tensor_tensor(flat, flat, tb, ALU.mult)),
                           ("dve", lambda e: e.memset(pt[:], 0.0))])
        turned, copied = k.sig("turned"), k.sig("pt_copied")
        with nc.Block() as block:
            @block.tensor
            def _(pe):
                for h in range(NCH):
                    for g in range(G):
                        mm = pe.transpose(ps[0:S2, h, g * P:(g + 1) * P], sc[:, h, g, :], k.ident[:])
                    mm.then_inc(turned.sem, 1)

            @block.scalar
            def _(act):
                for h in range(NCH):
                    act.wait_ge(turned.sem, turned.at(h + 1))
                    act.activation(pt[0:S2, h, :], ps[0:S2, h, :], ACT.Copy).then_inc(copied.sem, 1)
        turned.passed(NCH)
        copied.passed(NCH)
        tiles = []
        for h in range(NCH):
            for m in range(C):
                tiles.append(Tile([(ct[:, h // CPB, m * P:(m + 1) * P], pt[:, h, :])], "dve",
                                  add_bank(X[:, m, h * W:(h + 1) * W])))
        project(k, tiles)


def ternary(k, w, n):
    with ExitStack() as ctx:
        s = k.sb("tern_s", [P, 1], ctx=ctx)
        r = k.sb("tern_r", [P, 1], ctx=ctx)
        x = k.sb("tern_x", [P, n], ctx=ctx)
        total = P * n
        MAGIC = 12582912.0
        steps(k, "chain", [("dve", lambda e: e.tensor_reduce(s[:], w, AX.X, ALU.add, apply_absolute_value=True))])
        project(k, [Tile([(k.inv[:], s[:])], "dve", lambda e, bank: e.tensor_scalar(
            r[:], bank, D / total, 1e-8, ALU.mult, ALU.max), cols=1)])
        steps(k, "chain", [("dve", lambda e: e.reciprocal(r[:], r[:])),
                           ("dve", lambda e: e.tensor_scalar(x[:], w, r[:, 0:1], MAGIC, ALU.mult, ALU.add)),
                           ("dve", lambda e: e.tensor_scalar(x[:], x[:], MAGIC, 1.0, ALU.subtract, ALU.min)),
                           ("dve", lambda e: e.tensor_scalar(x[:], x[:], -1.0, None, ALU.max)),
                           ("dve", lambda e: e.tensor_tensor(x[:], x[:], w, ALU.subtract)),
                           ("dve", lambda e: e.tensor_tensor(w, w, x[:], ALU.add))])


def feed_forward(k, a):
    X = k.X
    FT = FF // P
    with ExitStack() as ctx:
        XN = k.sb("XN", [P, C, N], ctx=ctx)
        w1 = k.sb("w1", [P, C * FF], ctx=ctx)
        w2 = k.sb("w2", [P, FT * D], ctx=ctx)
        b1 = k.sb("b1", [P, FT], ctx=ctx)
        b2 = k.sb("b2", [P, C], ctx=ctx)
        norm(k, X, XN, loads=[(w1[:], a["ff_w1"]), (w2[:], a["ff_w2"]), (b1[:], a["ff_b1"]), (b2[:], a["ff_b2"])])
        ternary(k, w1[:], C * FF)
        ternary(k, w2[:], FT * D)
        hid = k.sb("ff_hid", [P, FT, N], ctx=ctx)
        tiles = []
        for h in range(NCH):
            cols = slice(h * W, (h + 1) * W)
            for f in range(FT):
                prods = [(w1[:, c * FF + f * P:c * FF + (f + 1) * P], XN[:, c, cols]) for c in range(C)]
                tiles.append(Tile(prods, "act", lambda e, bank, f=f, cols=cols: e.activation(
                    hid[:, f, cols], bank, ACT.Gelu, bias=b1[:, f:f + 1])))
        project(k, tiles)
        tiles = []
        for h in range(NCH):
            cols = slice(h * W, (h + 1) * W)
            for m in range(C):
                prods = [(w2[:, f * D + m * P:f * D + (m + 1) * P], hid[:, f, cols]) for f in range(FT)]
                tiles.append(Tile(prods, "dve", lambda e, bank, m=m, cols=cols: e.scalar_tensor_tensor(
                    X[:, m, cols], bank, b2[:, m:m + 1], X[:, m, cols], ALU.add, ALU.add)))
        project(k, tiles)


STAGES = [mamba, cross, decoder, linear, cross_one, feed_forward]


def build(nc, a, out, stages=None):
    ctx = ExitStack()
    with ctx:
        k = Core(nc, ctx)
        k.ps = ctx.enter_context(nc.psum_tensor("ps", [P, 8, W], F32))
        k.X = k.sb("X", [P, C, N])
        k.ident = k.sb("ident", [P, P])
        k.sel2 = k.sb("sel2", [P, DS], BF16)
        k.inv = k.sb("inv", [P, P])
        k.eps = k.sb("eps", [P, 2])
        k.b_rows = nc.dram_tensor("b_rows", (B, DS, T), F32).ap()
        k.ident16 = k.sb("ident16", [P, P], BF16)
        k.late_key = k.sb("late_key", [P, P], BF16)
        k.early_query = k.sb("early_query", [P, P], BF16)
        k.q_parts = nc.dram_tensor("q_parts", (3, D, T), BF16).ap()
        k.k_parts = nc.dram_tensor("k_parts", (3, D, T), BF16).ap()
        k.m_parts = nc.dram_tensor("m_parts", (3, H, T), BF16).ap()
        k.o_rows = nc.dram_tensor("o_rows", (H // 4, P, 2, T), F32).ap()
        k.zeros = k.sb("zeros", [P, D])
        k.xs = nc.dram_tensor("xs", (N + (E_ - 1) * P, D), F32).ap()
        k.ys = nc.dram_tensor("ys", (N + (E_ - 1) * P, D), F32).ap()
        with ExitStack() as setup:
            masks = k.sb("masks", [P, 2, P], ctx=setup)
            load(k, [(k.X[:], a["x"]), (k.ident[:], a["ident"]), (masks[:], a["masks"])])
            steps(k, "chain", [
                ("dve", lambda e: e.memset(k.inv[:], 1.0 / D)),
                ("dve", lambda e: e.memset(k.zeros[:], 0.0)),
                ("dve", lambda e: e.memset(k.eps[:, 0:1], EPS)),
                ("dve", lambda e: e.memset(k.eps[:, 1:2], EPS_F32)),
                ("dve", lambda e: e.tensor_copy(k.ident16[:], k.ident[:])),
                ("dve", lambda e: e.tensor_copy(k.late_key[:], masks[:, 0, :])),
                ("dve", lambda e: e.tensor_copy(k.early_query[:], masks[:, 1, :])),
                ("dve", lambda e: e.tensor_tensor(k.sel2[:], k.ident[:, 0:DS], k.ident[:, DS:P], ALU.add)),
            ])
        ring = [k.sig(n) for n in ("maxed", "swept", "weighed", "used", "o_taken", "o_stored0", "o_stored1")]
        with nc.Block() as block:
            @block.sync
            def _(sp):
                for s in ring:
                    sp.sem_inc(s.sem, 16)
        for s in ring:
            s.passed(16)
        for stage in (STAGES if stages is None else stages):
            stage(k, a)
        load(k, [(out, k.X[:])])


def channels_first(x):
    import numpy as np
    x = np.asarray(x)
    x = x.reshape(-1, x.shape[-1]).T
    return np.ascontiguousarray(x.reshape(-1, P, x.shape[-1]).transpose(1, 0, 2))


def rows_first(w):
    import numpy as np
    w = np.asarray(w)
    return np.ascontiguousarray(w.reshape(-1, P, w.shape[-1]).transpose(1, 0, 2))


def columns(*vs):
    import numpy as np
    return np.ascontiguousarray(np.stack([np.asarray(v).reshape(-1, P).T for v in vs], axis=-1))


def lay_out(i):
    import numpy as np
    g = {n: np.asarray(v) for n, v in i.items()}
    a = {}
    a["x"] = channels_first(g["x"])
    a["ident"] = np.eye(P, dtype=np.float32)
    wx = g["L0_attn_W_x"].T
    a["w_in"] = rows_first(g["L0_attn_W_in"].T)
    a["w_x"] = rows_first(np.concatenate([wx, wx[:, DR + DS:]], axis=1))
    a["w_dt"] = np.pad(g["L0_attn_W_dt"].T, ((0, P - DR), (0, 0)))
    a["w_out"] = rows_first(g["L0_attn_W_out"].T)
    cw = g["L0_attn_conv_w"]
    a["mamba_vec"] = columns(cw[:, 0, 0], cw[:, 0, 1], cw[:, 0, 2], cw[:, 0, 3], g["L0_attn_conv_b"],
                             g["L0_attn_b_dt"], g["L0_attn_Dp"])
    a["a_log"] = rows_first(g["L0_attn_A_log"])
    a["rms_w"] = columns(g["L0_attn_norm_w"])[:, :, 0]
    late = np.where(np.arange(P)[None, :] > np.arange(P)[:, None], NEG, 0.0).astype(np.float32)
    a["masks"] = np.stack([late, late.T], axis=1)
    a["ctx"] = channels_first(g["ctx_1024"])
    a["ctx_rows"] = g["ctx_1024"].transpose(1, 0, 2)
    a["mask"] = g["mask_BxS2_bf0"].astype(np.int32)
    for n in "qkvo":
        a["cross_" + n] = rows_first(g[f"L0_xattn_W_{n}"].T)
    half = DK // 2
    wq, wk, wv = np.split(g["L0_ffn_attn_w"], 3, axis=1)

    def turn(w):
        return w.reshape(D, H, 2, half)[:, :, ::-1, :].reshape(D, D)

    a["ffn_attn"] = rows_first(np.concatenate([wq, turn(wq), wk, turn(wk), wv], axis=1))
    a["ffn_proj"] = rows_first(g["L0_ffn_proj_w"])
    freq = (np.float32(1.0) / np.float32(10000.0) ** (np.arange(0, DK, 2, dtype=np.float32) / np.float32(DK)))
    angle = (np.arange(T, dtype=np.float32)[:, None] * freq.astype(np.float32)[None, :]).astype(np.float32)
    angle = np.concatenate([angle, angle], axis=1)
    sign = np.where(np.arange(DK) < half, -1.0, 1.0)
    cos = np.tile(np.cos(angle).T, (P // DK, 1))
    sin = np.tile((np.sin(angle) * sign).T, (P // DK, 1))
    a["rope"] = np.stack([cos, sin], axis=1).astype(np.float32)
    taps = g["L0_ffn_conv_w"]
    a["ffn_vec"] = columns(g["L0_ffn_ln1_w"], g["L0_ffn_ln1_b"], g["L0_ffn_ln2_w"], g["L0_ffn_ln2_b"],
                           taps[:, 0, 0], taps[:, 0, 1], taps[:, 0, 2])
    a["router"] = rows_first(g["L0_ffn_router_w"])
    a["before"] = np.triu(np.ones((P, P), np.float32), 1)
    a["tile_counts"] = np.tile(np.concatenate([np.arange(N // P) * P, np.arange(N // P + E_ - 1)]).astype(np.float32),
                               (P, 1))
    a["expert_wv"] = g["L0_ffn_expert_wv"].reshape(E_, C, P, 2 * FF).transpose(2, 0, 1, 3).reshape(P, -1)
    a["expert_proj"] = g["L0_ffn_expert_proj"].reshape(E_, FF // P, P, D).transpose(2, 0, 1, 3).reshape(P, -1)
    a["lin_qkv"] = rows_first(g["L1_attn_w_qkv"].T)
    a["lin_proj"] = rows_first(g["L1_attn_w_proj"].T)
    a["lin_bias"] = columns(g["L1_attn_b_proj"])[:, :, 0]
    a["same_head"] = np.kron(np.eye(P // DK), np.ones((DK, DK))).astype(np.float32)
    a["one_w"] = rows_first(g["L1_xattn_W"].T)
    a["one_bias"] = columns(g["L1_xattn_b"])[:, :, 0]
    a["ff_w1"] = rows_first(g["L1_ffn_W1"].T).reshape(P, -1)
    a["ff_w2"] = rows_first(g["L1_ffn_W2"].T).reshape(P, -1)
    a["ff_b1"] = columns(g["L1_ffn_b1"])[:, :, 0]
    a["ff_b2"] = columns(g["L1_ffn_b2"])[:, :, 0]
    return {n: np.ascontiguousarray(v) for n, v in a.items()}


def kernel(**inputs):
    import numpy as np
    import concourse.bacc as bacc
    from concourse.bass_utils import run_bass_kernel_spmd as run

    nc = bacc.Bacc("TRN2", target_bir_lowering=False, num_devices=1)
    arrays = lay_out(inputs)
    a = {n: nc.dram_tensor(f"in_{n}", v.shape, mybir.dt.from_np(v.dtype), kind="ExternalInput").ap()
         for n, v in arrays.items()}
    out = nc.dram_tensor("out", (P, C, N), F32, kind="ExternalOutput").ap()
    build(nc, a, out)
    r = run(nc, [{f"in_{n}": v for n, v in arrays.items()}], core_ids=[0])
    y = np.asarray(r.results[0]["out"])
    return np.ascontiguousarray(y.transpose(1, 0, 2).reshape(D, N).T).reshape(B, T, D)
```
